# Optimizing a Trainium2 kernel written in Bass

```python
import numpy as np
import jax
import jax.numpy as jnp

def _softmax(x, axis=-1):
    return jax.nn.softmax(x, axis=axis)

def _gelu(x):
    return jax.nn.gelu(x, approximate=True)

def _silu(x):
    return jax.nn.silu(x)

def _sigmoid(x):
    return jax.nn.sigmoid(x)

def _layernorm(x, axis=-1, eps=1e-05):
    m = jnp.mean(x, axis=axis, keepdims=True)
    v = jnp.var(x, axis=axis, keepdims=True)
    return (x - m) / jnp.sqrt(v + eps)

def _scatter_add(tgt, idx, src, axis=0):
    return tgt.at[idx].add(src)

def _segment_sum(src, seg, n):
    return jax.ops.segment_sum(src, seg, n)
kernel_name = 'mk_sandwich_d2_jaxref_r8_517e64'

def setup_inputs(seed: int=0):
    np.random.seed(seed)
    _w = jnp.asarray

    def _L0_attn_setup():
        import jax, jax.numpy as jnp
        import numpy as np
        NUM_HEADS = 16

        def _feature(x):
            return jax.nn.elu(x) + 1.0
        key = jax.random.key(seed)
        ks = jax.random.split(key, 9)
        B, N, E = (2, 256, 128)
        s = 1.0 / np.sqrt(E).astype(np.float32)
        inp = {'x': jax.random.normal(ks[0], (B, N, E), jnp.float32)}
        names = ['q', 'k', 'v', 'o']
        for i, n in enumerate(names):
            inp[f'W{n}'] = jax.random.normal(ks[1 + 2 * i], (E, E), jnp.float32) * s
            inp[f'b{n}'] = jax.random.normal(ks[2 + 2 * i], (E,), jnp.float32) * 0.01
        return inp
    _L0_attn_in = _L0_attn_setup()

    def _L0_ffn_setup():
        import jax, jax.numpy as jnp
        import numpy as np
        B, S, D = (2, 128, 128)
        H = 64
        E = 16
        K = 2
        HS = 2 * H
        ROUTE_SCALE = 1.0

        def _gated_mlp_act(y):
            u, g = jnp.split(y, 2, axis=-1)
            return u * jax.nn.silu(g)
        key = jax.random.key(seed)
        ks = jax.random.split(key, 6)
        s = 0.02
        return {'x': jax.random.normal(ks[0], (B, S, D), dtype=jnp.float32), 'Wg': jax.random.normal(ks[1], (E, D), dtype=jnp.float32) * s, 'W1': jax.random.normal(ks[2], (E, D, 2 * H), dtype=jnp.float32) * s, 'W2': jax.random.normal(ks[3], (E, H, D), dtype=jnp.float32) * s, 'Ws1': jax.random.normal(ks[4], (D, 2 * HS), dtype=jnp.float32) * s, 'Ws2': jax.random.normal(ks[5], (HS, D), dtype=jnp.float32) * s}
    _L0_ffn_in = _L0_ffn_setup()

    def _L1_attn_setup():
        import jax, jax.numpy as jnp
        import numpy as np
        B, L, D, E, N, DDELTA, DCONV = (4, 256, 128, 256, 16, 64, 4)
        EPS = 1e-05
        key = jax.random.key(seed)
        ks = jax.random.split(key, 12)

        def rn(k, shape, scale=0.02):
            return (jax.random.normal(k, shape) * scale).astype(jnp.float32)
        return {'resid': jax.random.normal(ks[0], (B, L, D), dtype=jnp.float32), 'norm_w': jnp.ones((D,), jnp.float32), 'skip_w': rn(ks[1], (E, D)), 'in_w': rn(ks[2], (E, D)), 'conv_w': rn(ks[3], (E, 1, DCONV), 0.1), 'conv_b': jnp.zeros((E,), jnp.float32), 'Wd1': rn(ks[4], (DDELTA, E)), 'Wd2_w': rn(ks[5], (E, DDELTA)), 'Wd2_b': rn(ks[6], (E,), 0.01), 'WB': rn(ks[7], (N, E)), 'WC': rn(ks[8], (N, E)), 'A_log': (jax.random.normal(ks[9], (E, N)) * 0.5).astype(jnp.float32), 'W_D': jnp.ones((E,), jnp.float32), 'out_w': rn(ks[10], (D, E))}
    _L1_attn_in = _L1_attn_setup()

    def _L1_ffn_setup():
        import jax, jax.numpy as jnp
        import numpy as np
        N_EMBED = 128
        HIDDEN = int(2 / 3 * 4 * N_EMBED)
        NUM_EXPERTS = 8
        TOP_K = 2
        key = jax.random.key(seed)
        ks = jax.random.split(key, 5)
        B, T, C, E, H = (2, 256, N_EMBED, NUM_EXPERTS, HIDDEN)
        s = 0.02
        return {'x': jax.random.normal(ks[0], (B, T, C), dtype=jnp.float32), 'gate_w': jax.random.normal(ks[1], (E, C), dtype=jnp.float32) * s, 'w1': jax.random.normal(ks[2], (E, H, C), dtype=jnp.float32) * s, 'w2': jax.random.normal(ks[3], (E, H, C), dtype=jnp.float32) * s, 'w3': jax.random.normal(ks[4], (E, C, H), dtype=jnp.float32) * s}
    _L1_ffn_in = _L1_ffn_setup()
    _d = {'L0_attn_x': _L0_attn_in['x'], 'L0_attn_Wq': _L0_attn_in['Wq'], 'L0_attn_bq': _L0_attn_in['bq'], 'L0_attn_Wk': _L0_attn_in['Wk'], 'L0_attn_bk': _L0_attn_in['bk'], 'L0_attn_Wv': _L0_attn_in['Wv'], 'L0_attn_bv': _L0_attn_in['bv'], 'L0_attn_Wo': _L0_attn_in['Wo'], 'L0_attn_bo': _L0_attn_in['bo'], 'L0_ffn_Wg': _L0_ffn_in['Wg'], 'L0_ffn_W1': _L0_ffn_in['W1'], 'L0_ffn_W2': _L0_ffn_in['W2'], 'L0_ffn_Ws1': _L0_ffn_in['Ws1'], 'L0_ffn_Ws2': _L0_ffn_in['Ws2'], 'L1_attn_norm_w': _L1_attn_in['norm_w'], 'L1_attn_skip_w': _L1_attn_in['skip_w'], 'L1_attn_in_w': _L1_attn_in['in_w'], 'L1_attn_conv_w': _L1_attn_in['conv_w'], 'L1_attn_conv_b': _L1_attn_in['conv_b'], 'L1_attn_Wd1': _L1_attn_in['Wd1'], 'L1_attn_Wd2_w': _L1_attn_in['Wd2_w'], 'L1_attn_Wd2_b': _L1_attn_in['Wd2_b'], 'L1_attn_WB': _L1_attn_in['WB'], 'L1_attn_WC': _L1_attn_in['WC'], 'L1_attn_A_log': _L1_attn_in['A_log'], 'L1_attn_W_D': _L1_attn_in['W_D'], 'L1_attn_out_w': _L1_attn_in['out_w'], 'L1_ffn_gate_w': _L1_ffn_in['gate_w'], 'L1_ffn_w1': _L1_ffn_in['w1'], 'L1_ffn_w2': _L1_ffn_in['w2'], 'L1_ffn_w3': _L1_ffn_in['w3']}
    _x0 = _d['L0_attn_x']
    _d['L0_attn_x'] = jax.random.normal(jax.random.fold_in(jax.random.key(seed), 1), (4, 1024, 128), dtype=_x0.dtype)
    del _x0
    return _d

def reference(L0_attn_x, L0_attn_Wq, L0_attn_bq, L0_attn_Wk, L0_attn_bk, L0_attn_Wv, L0_attn_bv, L0_attn_Wo, L0_attn_bo, L0_ffn_Wg, L0_ffn_W1, L0_ffn_W2, L0_ffn_Ws1, L0_ffn_Ws2, L1_attn_norm_w, L1_attn_skip_w, L1_attn_in_w, L1_attn_conv_w, L1_attn_conv_b, L1_attn_Wd1, L1_attn_Wd2_w, L1_attn_Wd2_b, L1_attn_WB, L1_attn_WC, L1_attn_A_log, L1_attn_W_D, L1_attn_out_w, L1_ffn_gate_w, L1_ffn_w1, L1_ffn_w2, L1_ffn_w3):

    def _L0_attn_ref(x, Wq, bq, Wk, bk, Wv, bv, Wo, bo):
        import jax, jax.numpy as jnp
        import numpy as np
        NUM_HEADS = 16

        def _feature(x):
            return jax.nn.elu(x) + 1.0
        B, N, E = x.shape
        H = NUM_HEADS
        d = E // H

        def proj(t, W, b):
            return t @ W.T + b

        def split_heads(t):
            return t.reshape(B, N, H, d).transpose(0, 2, 1, 3)
        q = _feature(split_heads(proj(x, Wq, bq)))
        k = _feature(split_heads(proj(x, Wk, bk)))
        v = split_heads(proj(x, Wv, bv))
        kv = jnp.cumsum(k[..., :, None] * v[..., None, :], axis=2)
        o = jnp.einsum('bhnd,bhnde->bhne', q, kv)
        o = o.transpose(0, 2, 1, 3).reshape(B, N, E)
        return o @ Wo.T + bo

    def _L0_ffn_ref(x, Wg, W1, W2, Ws1, Ws2):
        import jax, jax.numpy as jnp
        import numpy as np
        B, S, D = (2, 128, 128)
        H = 64
        E = 16
        K = 2
        HS = 2 * H
        ROUTE_SCALE = 1.0

        def _gated_mlp_act(y):
            u, g = jnp.split(y, 2, axis=-1)
            return u * jax.nn.silu(g)
        x_shape = x.shape
        xf = x.reshape(-1, D)
        scores = jax.nn.softmax(xf @ Wg.T, axis=-1)
        wk, idx = jax.lax.top_k(scores, K)
        wk = wk * ROUTE_SCALE
        cw = jnp.sum(jax.nn.one_hot(idx, E, dtype=xf.dtype) * wk[..., None], axis=1)
        h = _gated_mlp_act(jnp.einsum('td,edh->teh', xf, W1))
        z = jnp.einsum('te,teh,ehd->td', cw, h, W2)
        ys = _gated_mlp_act(xf @ Ws1) @ Ws2
        return (z + ys).reshape(x_shape)

    def _L1_attn_ref(resid, norm_w, skip_w, in_w, conv_w, conv_b, Wd1, Wd2_w, Wd2_b, WB, WC, A_log, W_D, out_w):
        import jax, jax.numpy as jnp
        import numpy as np
        B, L, D, E, N, DDELTA, DCONV = (4, 256, 128, 256, 16, 64, 4)
        EPS = 1e-05
        x = resid * jax.lax.rsqrt(jnp.mean(resid * resid, axis=-1, keepdims=True) + EPS) * norm_w
        skip = x @ skip_w.T
        x = x @ in_w.T
        xc = jnp.transpose(x, (0, 2, 1))
        xc = jax.lax.conv_general_dilated(xc, conv_w, window_strides=(1,), padding=[(DCONV - 1, 0)], dimension_numbers=('NCH', 'OIH', 'NCH'), feature_group_count=conv_w.shape[0])
        x = jnp.transpose(xc, (0, 2, 1)) + conv_b
        x = jax.nn.silu(x)
        A = -jnp.exp(A_log)
        delta = jax.nn.softplus(x @ Wd1.T @ Wd2_w.T + Wd2_b)
        Bm = x @ WB.T
        Cm = x @ WC.T

        def step(h, inp):
            x_l, d_l, B_l, C_l = inp
            A_bar = jnp.exp(d_l[:, :, None] * A)
            h = A_bar * h + (d_l * x_l)[:, :, None] * B_l[:, None, :]
            y_l = jnp.einsum('ben,bn->be', h, C_l)
            return (h, y_l)
        h0 = jnp.zeros((resid.shape[0], A.shape[0], A.shape[1]), x.dtype)
        xs = (jnp.swapaxes(x, 0, 1), jnp.swapaxes(delta, 0, 1), jnp.swapaxes(Bm, 0, 1), jnp.swapaxes(Cm, 0, 1))
        _, ys = jax.lax.scan(step, h0, xs)
        y = jnp.swapaxes(ys, 0, 1)
        y = y + x * W_D
        y = y * jax.nn.silu(skip)
        y = y @ out_w.T
        return resid + y

    def _L1_ffn_ref(x, gate_w, w1, w2, w3):
        import jax, jax.numpy as jnp
        import numpy as np
        N_EMBED = 128
        HIDDEN = int(2 / 3 * 4 * N_EMBED)
        NUM_EXPERTS = 8
        TOP_K = 2
        B, T, C = x.shape
        E = gate_w.shape[0]
        xt = x.reshape(-1, C)
        N = xt.shape[0]
        logits = jnp.einsum('nc,ec->ne', xt, gate_w)
        top_vals, top_idx = jax.lax.top_k(logits, TOP_K)
        top_w = jax.nn.softmax(top_vals.astype(jnp.float32), axis=-1).astype(x.dtype)
        route = jnp.zeros((N, E), dtype=x.dtype)
        route = route.at[jnp.arange(N)[:, None], top_idx].set(top_w)
        h1 = jnp.einsum('nc,ehc->enh', xt, w1)
        h2 = jnp.einsum('nc,ehc->enh', xt, w2)
        act = jax.nn.silu(h1) * h2
        expert_out = jnp.einsum('enh,ech->enc', act, w3)
        out = jnp.einsum('ne,enc->nc', route, expert_out)
        return out.reshape(B, T, C)
    x = L0_attn_x
    x = x + _layernorm(_L0_attn_ref(_layernorm(x, axis=-1), L0_attn_Wq, L0_attn_bq, L0_attn_Wk, L0_attn_bk, L0_attn_Wv, L0_attn_bv, L0_attn_Wo, L0_attn_bo), axis=-1)
    x = x + _layernorm(_L0_ffn_ref(_layernorm(x, axis=-1), L0_ffn_Wg, L0_ffn_W1, L0_ffn_W2, L0_ffn_Ws1, L0_ffn_Ws2), axis=-1)
    x = x + _layernorm(_L1_attn_ref(_layernorm(x, axis=-1), L1_attn_norm_w, L1_attn_skip_w, L1_attn_in_w, L1_attn_conv_w, L1_attn_conv_b, L1_attn_Wd1, L1_attn_Wd2_w, L1_attn_Wd2_b, L1_attn_WB, L1_attn_WC, L1_attn_A_log, L1_attn_W_D, L1_attn_out_w), axis=-1)
    x = x + _layernorm(_L1_ffn_ref(_layernorm(x, axis=-1), L1_ffn_gate_w, L1_ffn_w1, L1_ffn_w2, L1_ffn_w3), axis=-1)
    return x

_drawn_inputs = setup_inputs


def setup_inputs(seed=0):
    import zlib

    import numpy as np

    out = dict(_drawn_inputs(seed))
    spreads = {'L1_attn_norm_w': (1.0, 0.6), 'L1_attn_conv_b': (0.0, 0.8), 'L1_attn_W_D': (1.0, 0.6)}
    factors = {'L0_attn_bq': 3.138,
     'L0_attn_bk': 3.78,
     'L0_attn_bo': 64.0,
     'L1_attn_skip_w': 6.326,
     'L1_attn_in_w': 8.0,
     'L1_attn_conv_w': 8.0,
     'L1_attn_Wd1': 8.0,
     'L1_attn_Wd2_w': 8.0,
     'L1_attn_Wd2_b': 23.581,
     'L1_attn_WB': 8.0,
     'L1_attn_WC': 8.0,
     'L1_attn_A_log': 8.0,
     'L1_attn_out_w': 7.746}
    for name, (base, spread) in spreads.items():
        noise = np.random.default_rng([zlib.crc32(name.encode()), seed]).standard_normal(out[name].shape)
        drawn = base * np.exp(spread * noise) if base else spread * noise
        out[name] = jnp.asarray(drawn.astype(out[name].dtype))
    for name, factor in factors.items():
        out[name] = (out[name] * factor).astype(out[name].dtype)
    return out
```

```python
from contextlib import ExitStack

import concourse.bass as bass
from concourse import mybir

ALU = mybir.AluOpType
ACT = mybir.ActivationFunctionType
F32 = mybir.dt.float32
AX_X = mybir.AxisListType.X

P = 128
TILES = 32
BATCHES = 4
TB = 8
GT = 4
GROUPS = 8
GW = GT * P
EPS = 1e-5
HEADS, HD = 16, 8
E0, H0 = 16, 64
PAIRS = E0 // 2
BLK0 = PAIRS + 1
E1, H1 = 8, 341
CH = [(0, 128), (128, 128), (256, 85)]
NCH = len(CH)
BLK1 = E1 * NCH
N = 16
DD = 64
TAPS = 4
ARENA = 27800


def due(count):
    return not isinstance(count, int) or count > 0


def pipeline(eng, slots, peel, emit):
    for b in range(peel):
        emit(b, lambda s, lag, b=b: b * slots + s >= lag)
    with eng.Fori(peel, BATCHES) as b:
        emit(b, lambda s, lag: True)
    emit(BATCHES, lambda s, lag: s < lag)


def program(nc, A, out, stages=4):
    with ExitStack() as ctx:
        def sb(name, shape, dt=F32):
            return ctx.enter_context(nc.sbuf_tensor(name, shape, dt))

        def sem(name):
            return ctx.enter_context(nc.semaphore(name))

        X = sb("X", [P, TILES, P])
        MV = sb("MV", [P, TILES, 2])
        RS = sb("RS", [P, TILES])
        ident = sb("ident", [P, P])
        tri = sb("tri", [P, P])
        heads = sb("heads", [P, P])
        rev = sb("rev", [P, E0])
        ones = sb("ones", [1, P])
        mhalf = sb("mhalf", [P, GT])
        wqkv = sb("wqkv", [P, 3 * P])
        bqkv = sb("bqkv", [1, 3 * P])
        wo = sb("wo", [P, P])
        bo = sb("bo", [1, P])
        wg0 = sb("wg0", [P, E0])
        w1u = sb("w1u", [P, BLK0, P])
        w1g = sb("w1g", [P, BLK0, P])
        w2 = sb("w2", [P, BLK0, P])
        nw = sb("nw", [P, 1])
        wskip = sb("wskip", [P, 2 * P])
        win = sb("win", [P, 2 * P])
        taps = sb("taps", [P, 2, TAPS])
        cb = sb("cb", [P, 2])
        wd1 = sb("wd1", [P, 2, DD])
        wd2 = sb("wd2", [DD, 2 * P])
        bd2 = sb("bd2", [P, 2])
        wbc = sb("wbc", [P, 2, 2 * N])
        alog = sb("alog", [P, 2, N])
        aneg = sb("aneg", [P, 2, N])
        wdd = sb("wdd", [P, 2])
        wout = sb("wout", [P, 2, P])
        wg1 = sb("wg1", [P, E1])
        wa = sb("wa", [P, E1 * H1])
        wb = sb("wb", [P, E1 * H1])
        wc = sb("wc", [P, E1, NCH, P])

        ys = sb("ys", [P, 2, GT, P])
        tmp = sb("tmp", [P, GT, P])
        bny = sb("bny", [P, GT, 6])
        mvy = sb("mvy", [P, GT, 2])
        rsy = sb("rsy", [P, GT])
        vy = sb("vy", [P, GT])
        vx = sb("vx", [P, GT])
        bnx = sb("bnx", [P, GT, 6])
        mvx = sb("mvx", [P, GT, 2])
        eps = sb("eps", [P, GT])
        one = sb("one", [P, 2])
        carried = sb("carried", [P, 16])
        zs = sb("zs", [P, GT, P])

        arena = sb("arena", [P, ARENA])
        used = [0]

        def carve(*shape):
            n = 1
            for d in shape:
                n *= d
            ap = arena[:, used[0]:used[0] + n]
            used[0] += n
            assert used[0] <= ARENA, used[0]
            names = "abcde"[:len(shape)]
            if len(shape) == 1:
                return ap
            return ap.rearrange("p (" + " ".join(names) + ") -> p " + " ".join(names),
                                **{names[k]: shape[k] for k in range(1, len(shape))})

        az = carve(2, P)
        azT = carve(2, P)
        amn = carve(2, 2 * P)
        aex = carve(2, 2 * P)
        aphi = carve(2, 2 * P)
        av = carve(2, P)
        akv = carve(2, HEADS * HD * HD)
        aqT = carve(2, P)
        aprod = carve(HEADS * HD * HD)
        ared = carve(P)
        ao = carve(2, P)
        aoT = carve(2, P)
        asm = carve(P)
        used[0] = 0
        fzT = carve(2, GW)
        fsg = carve(2, GW)
        fa1 = carve(2, GW)
        fcw = carve(2, GT, E0)
        r_m = carve(GT)
        r_l = carve(GT, E0)
        r_ex = carve(GT, E0)
        r_p = carve(GT, E0)
        r_s = carve(GT)
        r_rs = carve(GT)
        r_eq = carve(GT, E0)
        r_oh = carve(2, GT, E0)
        r_l2 = carve(GT, E0)
        fact = carve(2, GW)
        fact1 = carve(2, NCH, GW)
        fwide = carve(2, GT, E0 * H0)
        used[0] = 0
        mxn = carve(GW)
        mxin = carve(2, TAPS - 1 + GW)
        mu = carve(2, GW)
        mxs = carve(2, 2, GW)
        msk = carve(2, 2, GW)
        md1 = carve(GW)
        mxb = carve(2, GW)
        mab = carve(2, GW)
        mex = carve(2, GW)
        mw = carve(2, GW)
        mln, mq = mab, mw
        mdl = carve(2, 2, GW)
        mdx = carve(2, 2, GW)
        mbc = carve(2, GT, 2 * N)
        mBs = carve(2, GW)
        mdB = carve(2, 2, GW)
        mh = carve(2, 2, GW)
        mhc = carve(N, 2)
        mP = carve(2, 2, GW)
        my = carve(2, GW)
        myg = my
        mres = carve(GT, P)
        mr = carve(5, GT)

        PS = ctx.enter_context(nc.psum_tensor("PS", [P, 8, 512], F32))

        def bank(k, n=512, p=P):
            return PS[0:p, k, 0:n]

        def bank_tiles(k, w=P):
            return PS[:, k, 0:GT * w].rearrange("p (t w) -> p t w", w=w)

        s_x = [sem(f"s_x{b}") for b in range(BATCHES)]
        s_c = [sem(f"s_c{i}") for i in range(4)]
        s_out = sem("s_out")
        x_stats, x_rstd, vx_ok = sem("x_stats"), sem("x_rstd"), sem("vx_ok")
        ys_ok, y_stats, y_rstd, vy_ok = sem("ys_ok"), sem("y_stats"), sem("y_rstd"), sem("vy_ok")
        ep = sem("ep")
        pool_const = sem("pool_const")
        ATT = {n: sem(f"a_{n}") for n in (
            "ln_ready", "ln_transposed", "lnT_copied", "qk_ready", "v_ready", "min_ready", "exp_ready", "v_copied",
            "feature_ready", "kv_ready", "q_transposed", "qT_copied", "kv_cumulated", "state_added",
            "product_ready", "product_summed", "state_masked", "o_ready", "o_transposed", "oT_copied", "y_ready")}
        F = [{n: sem(f"f{m}_{n}") for n in (
            "ln_ready", "ln_transposed", "lnT_copied", "logits_ready", "logits_shifted", "exp_ready",
            "weights_ready", "routing_step", "up_gate_ready", "silu_ready", "product_ready", "act_ready",
            "block_added", "expert_ready", "expert_combined", "weights_widened")} for m in range(2)]
        MAM = {n: sem(f"m_{n}") for n in (
            "scale_step", "ln_ready", "ln_transposed", "lnT_copied", "in_proj_ready", "in_proj_copied",
            "carry_ready", "conv_step", "skip_ready", "skip_silu_ready", "x_silu_ready", "d1_ready", "d1_copied",
            "bc_ready", "bc_copied", "d2_ready", "d2_copied", "abs_ready", "exp_ready", "one_plus_exp_ready",
            "log_ready", "correction_ready", "delta_partly_ready", "delta_ready", "delta_x_ready", "b_spread",
            "b_copied", "c_spread", "delta_x_b_ready", "decay_ready", "half_scanned", "state_c_ready",
            "state_added", "y_ready", "gated_ready", "out_proj_ready", "residual_ready", "a_ready", "state_kept")}
        EPN = 4

        def group(T, g):
            return T[:, bass.ds(GT * g, GT)]

        def xt(i):
            return X[:, bass.ds(i, 1), :].rearrange("p a d -> p (a d)")

        def mean(i):
            return MV[:, bass.ds(i, 1), 0:1].rearrange("p a c -> p (a c)")

        def wide(ap, n):
            return ap.rearrange("p (t o) -> p t o", o=1).to_broadcast([P, GT, n])

        carriers = [0, 0]

        def pool_carrier():
            k = carriers[0] = (carriers[0] + 1) % 8
            nc.gpsimd.tensor_tensor(carried[:, k:k + 1], one[:, 0:1], one[:, 0:1], ALU.mult)

        def dve_carrier():
            k = carriers[1] = (carriers[1] + 1) % 8
            nc.vector.memset(carried[:, 8 + k:9 + k], 0.0)

        def pool_x_rstd(pool, st, g):
            n = GROUPS * st + g + 1
            pool.wait_ge(x_stats, n)
            pool.tensor_tensor(vx[:, :], mvx[:, :, 1], eps[:, :], ALU.add).then_inc(vx_ok, 1)
            pool.tensor_copy(group(MV, g), mvx[:, :, :])
            pool.wait_ge(vx_ok, n)
            pool_carrier()
            pool.tensor_tensor(group(RS, g), vx[:, :], mhalf[:, :], ALU.pow).then_inc(x_rstd, 1)

        def pool_y_rstd(pool, st, g):
            n = GROUPS * st + g + 1
            pool.wait_ge(y_stats, n)
            pool.tensor_tensor(vy[:, :], mvy[:, :, 1], eps[:, :], ALU.add).then_inc(vy_ok, 1)
            pool.wait_ge(vy_ok, n)
            pool.tensor_tensor(rsy[:, :], vy[:, :], mhalf[:, :], ALU.pow).then_inc(y_rstd, 1)

        def ep_count(st, g, c):
            per = EPN if st < stages - 1 else EPN - 1
            return EPN * GROUPS * st + per * g + c

        def stage_begins(eng, st):
            if st:
                eng.wait_ge(ep, ep_count(st - 1, GROUPS, 0))

        def dve_y_stats(dve, st, g, par):
            dve.wait_ge(ys_ok, GROUPS * st + g + 1)
            if due(GROUPS * st + g):
                dve.wait_ge(y_stats, GROUPS * st + g)
            for t in range(GT):
                i = dve.bn_stats(bny[:, t, :], ys[:, par, t, :])
            i.then_inc(ep, 1)
            dve.wait_ge(ep, ep_count(st, g, 1))
            dve_carrier()
            for t in range(GT):
                i = dve.bn_aggr(mvy[:, t, :], bny[:, t, :])
            i.then_inc(y_stats, 1)

        def dve_x_update(dve, st, g, par):
            dve.wait_ge(y_rstd, GROUPS * st + g + 1)
            for t in range(GT):
                i = dve.tensor_scalar(tmp[:, t, :], ys[:, par, t, :], mvy[:, t, 0:1], rsy[:, t:t + 1],
                                      ALU.subtract, ALU.mult)
            i.then_inc(ep, 1)
            dve.wait_ge(ep, ep_count(st, g, 2))
            dve.tensor_tensor(group(X, g), group(X, g), tmp[:, :, :], ALU.add).then_inc(ep, 1)
            if st < stages - 1:
                dve_x_stats(dve, g, ep, ep_count(st, g, 4), GROUPS * (st + 1) + g, (ep, ep_count(st, g, 3)))

        def dve_x_stats(dve, g, s, n, rstd_before, *before):
            if due(rstd_before):
                dve.wait_ge(x_stats, rstd_before)
            for before_sem, before_n in before:
                dve.wait_ge(before_sem, before_n)
            dve_carrier()
            for t in range(GT):
                i = dve.bn_stats(bnx[:, t, :], xt(GT * g + t))
            i.then_inc(s, 1)
            dve.wait_ge(s, n)
            if due(rstd_before):
                dve.wait_ge(x_rstd, rstd_before)
            dve_carrier()
            for t in range(GT):
                i = dve.bn_aggr(mvx[:, t, :], bnx[:, t, :])
            i.then_inc(x_stats, 1)

        def dve_ln(dve, dst, i):
            return dve.tensor_scalar(dst, xt(i), mean(i), RS[:, bass.ds(i, 1)], ALU.subtract, ALU.mult)

        consts = (
            (("ident", ident), ("wqkv", wqkv), ("bqkv", bqkv), ("tri", tri), ("heads", heads), ("wo", wo), ("bo", bo)),
            (("rev", rev), ("wg0", wg0), ("w1u", w1u), ("w1g", w1g), ("w2", w2)),
            (("nw", nw), ("wskip", wskip), ("win", win), ("cb", cb), ("wd2", wd2), ("bd2", bd2), ("wdd", wdd),
             ("taps", taps), ("wd1", wd1), ("wbc", wbc), ("alog", alog), ("wout", wout)),
            (("wg1", wg1), ("wa", wa), ("wb", wb), ("wc", wc)),
        )

        def const_wait(eng, st):
            eng.wait_ge(s_c[st], 16 * len(consts[st]))

        def full(t):
            return t[tuple(slice(None) for _ in t.shape)]

        block = ctx.enter_context(nc.Block())

        @block.sync
        def _(sp):
            for b in range(BATCHES):
                sp.dma_start(X[:, TB * b:TB * b + TB, :], A["x"][b].rearrange("(t p) d -> p t d", p=P)).then_inc(s_x[b], 16)
                if b == 0:
                    for name, dst in consts[0]:
                        sp.dma_start(full(dst), A[name]).then_inc(s_c[0], 16)
            for st in range(1, 4):
                for name, dst in consts[st]:
                    sp.dma_start(full(dst), A[name]).then_inc(s_c[st], 16)
            for g in range(GROUPS):
                sp.wait_ge(ep, ep_count(stages - 1, g, 3))
                sp.dma_start(out.rearrange("b (t p) d -> p (b t) d", p=P)[:, GT * g:GT * g + GT, :],
                             X[:, GT * g:GT * g + GT, :]).then_inc(s_out, 16)
            sp.wait_ge(s_out, 16 * GROUPS)

        @block.gpsimd
        def _(pool):
            pool.memset(ones[:, :], 1.0)
            pool.memset(eps[:, :], EPS)
            pool.memset(one[:, :], 1.0)
            pool.memset(mhalf[:, :], -0.5).then_inc(pool_const, 1)
            pool.wait_ge(pool_const, 1)
            for g in range(GROUPS):
                pool_x_rstd(pool, 0, g)

            def attention(b, ok):
                for s in range(TB):
                    if ok(s, 1):
                        i, q = TB * b + s - 1, (s - 1) % 2
                        pool.wait_ge(ATT["feature_ready"], i + 1)
                        pool.wait_ge(ATT["v_copied"], i + 1)
                        if due(i - 1):
                            pool.wait_ge(ATT["kv_cumulated"], i - 1)
                        k4 = aphi[:, q, P:2 * P].rearrange("p (h o d) -> p h o d", h=HEADS, o=1)
                        v4 = av[:, q, :].rearrange("p (h e o) -> p h e o", h=HEADS, o=1)
                        shape = [P, HEADS, HD, HD]
                        pool.tensor_tensor(akv[:, q, :].rearrange("p (h e d) -> p h e d", e=HD, d=HD),
                                           k4.to_broadcast(shape), v4.to_broadcast(shape), ALU.mult).then_inc(ATT["kv_ready"], 1)
                    if ok(s, 4) and (s - 4) % GT == GT - 1:
                        g = (TB // GT) * b + (s - 4 - (GT - 1)) // GT
                        pool_y_rstd(pool, 0, g)
                        if stages > 1:
                            pool_x_rstd(pool, 1, g)
            pool_ep_lag = 4
            pipeline(pool, TB, 1, attention)

            def moe(st, m):
                f = F[m]

                def emit(b, ok):
                    for s in range(2):
                        g = 2 * b + s
                        if ok(s, 2):
                            pool_y_rstd(pool, st, g - 2)
                            if st < stages - 1:
                                pool_x_rstd(pool, st + 1, g - 2)
                        if m == 0 and ok(s, 0):
                            pool.wait_ge(f["weights_ready"], g + 1)
                            if due(BLK0 * (g - 1)):
                                pool.wait_ge(f["up_gate_ready"], BLK0 * (g - 1))
                            for t in range(GT):
                                i = pool.tensor_tensor(
                                    fwide[:, s % 2, t].rearrange("p (e u) -> p e u", u=H0),
                                    fcw[:, s % 2, t].rearrange("p (e o) -> p e o", o=1).to_broadcast([P, E0, H0]),
                                    one[:, 0:1].rearrange("p (a b) -> p a b", b=1).to_broadcast([P, E0, H0]), ALU.mult)
                            i.then_inc(f["weights_widened"], 1)
                stage_begins(pool, st)
                pipeline(pool, 2, 2, emit)

            def mamba_prep(s, g, n):
                if n == 0:
                    pool.wait_ge(x_rstd, GROUPS * 2 + g + 1)
                    if due(g):
                        pool.wait_ge(MAM["ln_ready"], g)
                    pool_carrier()
                    steps = (lambda: pool.tensor_tensor(mr[:, 0, :], group(RS, g), group(RS, g), ALU.mult),
                             lambda: pool.tensor_tensor(mr[:, 1, :], mr[:, 0, :], group(MV, g)[:, :, 1], ALU.mult),
                             lambda: pool.tensor_tensor(mr[:, 2, :], mr[:, 1, :], eps[:, :], ALU.add),
                             lambda: pool.tensor_tensor(mr[:, 3, :], mr[:, 2, :], mhalf[:, :], ALU.pow),
                             lambda: pool.tensor_tensor(mr[:, 4, :], mr[:, 3, :], group(RS, g), ALU.mult))
                    for c, step in enumerate(steps):
                        step().then_inc(MAM["scale_step"], 1)
                        pool.wait_ge(MAM["scale_step"], 5 * g + c + 1)
                        pool_carrier()
                if n == 1:
                    if due(6 * g):
                        pool.wait_ge(MAM["conv_step"], 6 * g)
                    pool_carrier()
                    if s == 0:
                        pool.memset(mxin[:, :, 0:TAPS - 1], 0.0).then_inc(MAM["carry_ready"], 1)
                    else:
                        pool.tensor_copy(mxin[:, :, 0:TAPS - 1], mxin[:, :, GW:GW + TAPS - 1]).then_inc(MAM["carry_ready"], 1)
                if n == 13:
                    pool.wait_ge(MAM["delta_ready"], g + 1)
                    pool.tensor_tensor(mdx[:, s % 2], mdl[:, s % 2], mxs[:, s % 2], ALU.mult).then_inc(MAM["delta_x_ready"], 1)

            def pool_dB(g, par, n):
                kk = N * g + n
                if n == 0:
                    pool.wait_ge(MAM["delta_x_ready"], g + 1)
                pool.wait_ge(MAM["b_copied"], kk + 1)
                if due(2 * (kk - 1)):
                    pool.wait_ge(MAM["half_scanned"], 2 * (kk - 1))
                pool.tensor_tensor(mdB[:, n % 2], mdx[:, par],
                                   mBs[:, n % 2, :].rearrange("p (o t) -> p o t", o=1).to_broadcast([P, 2, GW]),
                                   ALU.mult).then_inc(MAM["delta_x_b_ready"], 1)

            def keep_state(b, n):
                pool.wait_ge(MAM["half_scanned"], 2 * (N * 2 * b + n + 1))
                pool.tensor_tensor(mhc[:, n, :], mh[:, n % 2, :, GW - 1], one[:, :], ALU.mult).then_inc(MAM["state_kept"], 1)

            def mamba_post(s, g, n):
                if n == 1:
                    pool.wait_ge(MAM["y_ready"], g + 1)
                    if due(g):
                        pool.wait_ge(MAM["out_proj_ready"], g)
                    pool.tensor_tensor(myg[:, :, :], my[:, :, :], msk[:, s % 2], ALU.mult).then_inc(MAM["gated_ready"], 1)
                if n == 13:
                    pool_y_rstd(pool, 2, g)
                if n == 15 and stages > 3:
                    pool_x_rstd(pool, 3, g)

            def mamba(b, ok):
                for s in range(2):
                    g = 2 * b + s
                    for n in range(N):
                        if ok(s, 2):
                            mamba_post(s, g - 2, n)
                        if ok(s, 0):
                            mamba_prep(s, g, n)
                        if s == 1 and ok(s, 1) and n > 0:
                            keep_state(b, n - 1)
                        if ok(s, 1) and n < N - 1:
                            pool_dB(g - 1, (s - 1) % 2, n + 1)
                        if ok(s, 0) and n == N - 1:
                            pool_dB(g, s % 2, 0)
                    if s == 1 and ok(s, 1):
                        keep_state(b, N - 1)

            if stages > 1:
                moe(1, 0)
            if stages > 2:
                stage_begins(pool, 2)
                pool.wait_ge(MAM["a_ready"], 1)
                pool.tensor_scalar(aneg[:, :, :], aneg[:, :, :], -1.0, None, ALU.mult).then_inc(MAM["a_ready"], 1)
                pipeline(pool, 2, 2, mamba)
            if stages > 3:
                moe(3, 1)

        @block.scalar
        def _(act):
            def attention(b, ok):
                for s in range(TB):
                    q = s % 2
                    i = TB * b + s
                    if ok(s, 0):
                        act.wait_ge(ATT["ln_transposed"], i + 1)
                        if due(i - 1):
                            act.wait_ge(ATT["v_ready"], i - 1)
                        act.activation(azT[:, q, :], bank(0, P), ACT.Copy).then_inc(ATT["lnT_copied"], 1)
                    if ok(s, 1):
                        act.wait_ge(ATT["q_transposed"], i)
                        if due(i - 2):
                            act.wait_ge(ATT["state_added"], i - 2)
                        act.activation(aqT[:, 1 - q, :], bank(2, P), ACT.Copy).then_inc(ATT["qT_copied"], 1)
                    if ok(s, 3):
                        act.wait_ge(ATT["o_transposed"], i - 2)
                        if due(i - 4):
                            act.wait_ge(ATT["y_ready"], i - 4)
                        act.activation(aoT[:, 1 - q, :], bank(0, P), ACT.Copy).then_inc(ATT["oT_copied"], 1)
                    if ok(s, 0):
                        act.wait_ge(ATT["v_ready"], i + 1)
                        if due(i - 1):
                            act.wait_ge(ATT["kv_ready"], i - 1)
                        act.activation(av[:, q, :], bank(2, P), ACT.Copy).then_inc(ATT["v_copied"], 1)
                        act.wait_ge(ATT["min_ready"], i + 1)
                        if due(i - 1):
                            act.wait_ge(ATT["feature_ready"], i - 1)
                        act.activation(aex[:, q, :], amn[:, q, :], ACT.Exp).then_inc(ATT["exp_ready"], 1)
                    if ok(s, 3) and (s - 3) % GT == GT - 1:
                        g = (TB // GT) * b + (s - 3 - (GT - 1)) // GT
                        act.wait_ge(ATT["y_ready"], i - 2)
                        if due(ep_count(0, g - 1, 2)):
                            act.wait_ge(ep, ep_count(0, g - 1, 2))
                        act.activation(ys[:, ((s - 3) // GT) % 2], bank_tiles(7), ACT.Copy).then_inc(ys_ok, 1)
            const_wait(act, 2)
            act.activation(aneg[:, :, :], alog[:, :, :], ACT.Exp).then_inc(MAM["a_ready"], 1)
            pipeline(act, TB, 1, attention)

            def moe_prep(st, m, s, g, k):
                f = F[m]
                if k == 1:
                    act.wait_ge(f["ln_transposed"], g + 1)
                    if due((BLK0, BLK1)[m] * (g - 1)):
                        act.wait_ge(f["up_gate_ready"], (BLK0, BLK1)[m] * (g - 1))
                    act.activation(fzT[:, s % 2, :], bank(0), ACT.Copy).then_inc(f["lnT_copied"], 1)
                if k == 4:
                    E = (E0, E1)[m]
                    act.wait_ge(f["logits_shifted"], g + 1)
                    act.activation(r_ex[:, :, 0:E], r_l[:, :, 0:E], ACT.Exp).then_inc(f["exp_ready"], 1)

            def moe(st, m):
                f, B = F[m], (BLK0, BLK1)[m]

                def emit(b, ok):
                    for s in range(2):
                        g = 2 * b + s
                        for k in range(B):
                            if ok(s, 1):
                                kk, par = B * (g - 1) + k, (B * (s - 1) + k) % 2
                                act.wait_ge(f["up_gate_ready"], kk + 1)
                                if due(kk - 1):
                                    act.wait_ge(f["act_ready"], kk - 1)
                                act.activation(fsg[:, par, :], bank(4 + par), ACT.Silu).then_inc(f["silu_ready"], 1)
                            if ok(s, 0):
                                moe_prep(st, m, s, g, k)
                        if m == 0 and ok(s, 1):
                            act.wait_ge(f["block_added"], B * g)
                            act.wait_ge(ep, ep_count(st, g - 3, 2))
                            act.activation(ys[:, (s - 1) % 2], bank_tiles(7), ACT.Copy).then_inc(ys_ok, 1)
                stage_begins(act, st)
                pipeline(act, 2, 2, emit)

            def mamba_B(g, n):
                kk = N * g + n
                act.wait_ge(MAM["b_spread"], kk + 1)
                if due(kk - 1):
                    act.wait_ge(MAM["delta_x_b_ready"], kk - 1)
                act.activation(mBs[:, n % 2, :], bank(3), ACT.Copy).then_inc(MAM["b_copied"], 1)

            def mamba_prep(s, g, n):
                if n == 1:
                    act.wait_ge(MAM["ln_transposed"], g + 1)
                    if due(2 * g):
                        act.wait_ge(MAM["skip_ready"], 2 * g)
                    act.activation(mxn, bank(6), ACT.Copy, scale=nw[:, 0:1]).then_inc(MAM["lnT_copied"], 1)
                if n in (2, 3):
                    h = n - 2
                    act.wait_ge(MAM["in_proj_ready"], 2 * g + h + 1)
                    act.wait_ge(MAM["carry_ready"], g + 1)
                    act.activation(mxin[:, h, TAPS - 1:TAPS - 1 + GW], bank(7 - h), ACT.Copy)
                    act.activation(mu[:, h, :], bank(7 - h), ACT.Identity, bias=cb[:, h:h + 1],
                                   scale=taps[:, h, TAPS - 1:TAPS]).then_inc(MAM["in_proj_copied"], 1)
                if n == 6:
                    if due(g - 1):
                        act.wait_ge(MAM["gated_ready"], g - 1)
                    for h in range(2):
                        act.wait_ge(MAM["skip_ready"], 2 * g + h + 1)
                        act.activation(msk[:, s % 2, h, :], bank(7 - h), ACT.Silu).then_inc(MAM["skip_silu_ready"], 1)
                    act.wait_ge(MAM["conv_step"], 6 * g + 6)
                    if due(g - 1):
                        act.wait_ge(MAM["y_ready"], g - 1)
                    act.activation(mxs[:, s % 2], mu[:, :, :], ACT.Silu).then_inc(MAM["x_silu_ready"], 1)
                if n == 7:
                    act.wait_ge(MAM["d1_ready"], g + 1)
                    if due(2 * g):
                        act.wait_ge(MAM["d2_ready"], 2 * g)
                    act.activation(md1[0:DD, :], bank(7, GW, DD), ACT.Copy).then_inc(MAM["d1_copied"], 1)
                    act.wait_ge(MAM["bc_ready"], g + 1)
                    if due(N * (g - 1)):
                        act.wait_ge(MAM["state_c_ready"], N * (g - 1))
                    act.activation(mbc[:, s % 2], bank_tiles(6, 2 * N), ACT.Copy).then_inc(MAM["bc_copied"], 1)
                if n == 8:
                    if due(g):
                        act.wait_ge(MAM["delta_partly_ready"], g)
                    for h in range(2):
                        act.wait_ge(MAM["d2_ready"], 2 * g + h + 1)
                        act.activation(mxb[:, h, :], bank(7 - h), ACT.Identity, bias=bd2[:, h:h + 1]).then_inc(MAM["d2_copied"], 1)
                if n == 9:
                    act.wait_ge(MAM["d2_copied"], 2 * g + 2)
                    if due(g):
                        act.wait_ge(MAM["delta_ready"], g)
                    act.activation(mab[:, :, :], mxb[:, :, :], ACT.Abs).then_inc(MAM["abs_ready"], 1)
                    act.wait_ge(MAM["abs_ready"], g + 1)
                    act.activation(mex[:, :, :], mab[:, :, :], ACT.Exp, scale=-1.0).then_inc(MAM["exp_ready"], 1)
                    act.wait_ge(MAM["exp_ready"], g + 1)
                    act.activation(mw[:, :, :], mex[:, :, :], ACT.Copy, bias=1.0).then_inc(MAM["one_plus_exp_ready"], 1)
                    act.wait_ge(MAM["one_plus_exp_ready"], g + 1)
                    act.activation(mln[:, :, :], mw[:, :, :], ACT.Ln).then_inc(MAM["log_ready"], 1)

            def mamba(b, ok):
                for s in range(2):
                    g = 2 * b + s
                    for n in range(N):
                        if ok(s, 1):
                            for h in range(2):
                                kk = N * (g - 1) + n
                                act.wait_ge(MAM["delta_ready"], g)
                                if due(2 * kk - 1 + h):
                                    act.wait_ge(MAM["half_scanned"], 2 * kk - 1 + h)
                                act.activation(bank(4 + h), mdl[:, (s - 1) % 2, h, :], ACT.Exp,
                                               scale=aneg[:, h, n:n + 1]).then_inc(MAM["decay_ready"], 1)
                            if n < N - 1:
                                mamba_B(g - 1, n + 1)
                        if ok(s, 0):
                            mamba_prep(s, g, n)
                            if n == N - 1:
                                mamba_B(g, 0)

            if stages > 1:
                moe(1, 0)
            if stages > 2:
                stage_begins(act, 2)
                act.wait_ge(MAM["a_ready"], 2)
                pipeline(act, 2, 2, mamba)
            if stages > 3:
                moe(3, 1)

        @block.vector
        def _(dve):
            for g in range(GROUPS):
                dve.wait_ge(s_x[g // 2], 16)
                dve_x_stats(dve, g, ATT["product_summed"], g + 1, g)

            def attention(b, ok):
                for s in range(TB):
                    q = s % 2
                    if ok(s, 0):
                        i = TB * b + s
                        if s % GT == 0:
                            dve.wait_ge(x_rstd, (TB // GT) * b + s // GT + 1)
                        if due(i - 1):
                            dve.wait_ge(ATT["ln_transposed"], i - 1)
                        dve_ln(dve, az[:, q, :], i).then_inc(ATT["ln_ready"], 1)
                    if ok(s, 1):
                        i = TB * b + s - 1
                        dve.wait_ge(ATT["exp_ready"], i + 1)
                        if due(i - 1):
                            dve.wait_ge(ATT["kv_ready"], i - 1)
                        if due(i - 1):
                            dve.wait_ge(ATT["product_ready"], i - 1)
                        dve.scalar_tensor_tensor(aphi[:, 1 - q, :], bank(1, 2 * P), 0.0, aex[:, 1 - q, :],
                                                 ALU.max, ALU.add).then_inc(ATT["feature_ready"], 1)
                    if ok(s, 2):
                        i = TB * b + s - 2
                        dve.wait_ge(ATT["kv_cumulated"], i + 1)
                        q4 = aphi[:, q, 0:P].rearrange("p (h o d) -> p h o d", h=HEADS, o=1)
                        dve.tensor_tensor(aprod.rearrange("p (h e d) -> p h e d", e=HD, d=HD),
                                          PS[:, 3:5, :].rearrange("p b (h e d) -> p (b h) e d", e=HD, d=HD),
                                          q4.to_broadcast([P, HEADS, HD, HD]), ALU.mult).then_inc(ATT["product_ready"], 1)
                        dve.wait_ge(ATT["state_added"], i + 1)
                        dve.tensor_tensor(asm, bank(5, P), heads[:, :], ALU.mult).then_inc(ATT["state_masked"], 1)
                        dve.wait_ge(ATT["product_ready"], i + 1)
                        dve.tensor_reduce(ared, aprod.rearrange("p (c d) -> p c d", d=HD), AX_X, ALU.add)\
                           .then_inc(ATT["product_summed"], 1)
                        dve.wait_ge(ATT["product_summed"], GROUPS + i + 1)
                        if due(i - 1):
                            dve.wait_ge(ATT["o_transposed"], i - 1)
                        if s == 2:
                            dve.tensor_copy(ao[:, q, :], ared).then_inc(ATT["o_ready"], 1)
                        else:
                            dve.tensor_tensor(ao[:, q, :], bank(6, P), ared, ALU.add).then_inc(ATT["o_ready"], 1)
                    if ok(s, 0):
                        i = TB * b + s
                        dve.wait_ge(ATT["qk_ready"], i + 1)
                        if due(i - 1):
                            dve.wait_ge(ATT["exp_ready"], i - 1)
                        dve.tensor_scalar(amn[:, q, :], bank(1, 2 * P), 0.0, None, ALU.min).then_inc(ATT["min_ready"], 1)
                    if ok(s, 4) and (s - 4) % GT == GT - 1:
                        g = (TB // GT) * b + (s - 4 - (GT - 1)) // GT
                        dve_y_stats(dve, 0, g, ((s - 4) // GT) % 2)
                        dve_x_update(dve, 0, g, ((s - 4) // GT) % 2)
            const_wait(dve, 0)
            pipeline(dve, TB, 1, attention)

            def routing(m, s, g, part):
                f, E = F[m], (E0, E1)[m]
                R = 16
                c = [0 if part == 0 else 1]

                def step(i):
                    i.then_inc(f["routing_step"], 1)
                    c[0] += 1
                    dve.wait_ge(f["routing_step"], R * g + c[0])

                def v(ap):
                    return ap[:, :, 0:E]
                lv, ex, p, eq, l2 = v(r_l), v(r_ex), v(r_p), v(r_eq), v(r_l2)
                rank = rev[:, E0 - E:E0].rearrange("p (o e) -> p o e", o=1).to_broadcast([P, GT, E])
                if part == 0:
                    dve.wait_ge(f["logits_ready"], g + 1)
                    if due(g):
                        dve.wait_ge(f["weights_ready"], g)
                    step(dve.tensor_reduce(r_m, bank_tiles(1, E), AX_X, ALU.max))
                    dve.tensor_tensor(lv, bank_tiles(1, E), wide(r_m, E), ALU.subtract).then_inc(f["logits_shifted"], 1)
                    return
                dve.wait_ge(f["exp_ready"], g + 1)
                sel = lv
                if m == 0:
                    step(dve.tensor_reduce(r_s, ex, AX_X, ALU.add))
                    step(dve.reciprocal(r_rs, r_s))
                    step(dve.tensor_tensor(p, ex, wide(r_rs, E), ALU.mult))
                    sel = p
                for j in range(2):
                    step(dve.tensor_reduce(r_m, sel, AX_X, ALU.max))
                    step(dve.tensor_tensor(eq, sel, wide(r_m, E), ALU.is_ge))
                    step(dve.tensor_tensor(eq, eq, rank, ALU.mult))
                    step(dve.tensor_reduce(r_m, eq, AX_X, ALU.max))
                    step(dve.tensor_tensor(v(r_oh[:, j]), rank, wide(r_m, E), ALU.is_equal))
                    if j == 0:
                        step(dve.scalar_tensor_tensor(l2, v(r_oh[:, 0]), -1e30, sel, ALU.mult, ALU.add))
                        sel = l2
                step(dve.tensor_tensor(eq, v(r_oh[:, 0]), v(r_oh[:, 1]), ALU.add))
                if m == 0:
                    dve.tensor_tensor(v(fcw[:, s % 2]), eq, p, ALU.mult).then_inc(f["weights_ready"], 1)
                else:
                    step(dve.tensor_tensor(eq, eq, ex, ALU.mult))
                    step(dve.tensor_reduce(r_s, eq, AX_X, ALU.add))
                    step(dve.reciprocal(r_rs, r_s))
                    dve.tensor_tensor(v(fcw[:, s % 2]), eq, wide(r_rs, E), ALU.mult).then_inc(f["weights_ready"], 1)
                assert c[0] == R

            def moe0(b, ok):
                f = F[0]
                for s in range(2):
                    g = 2 * b + s
                    for k in range(BLK0):
                        if ok(s, 0) and k == 0:
                            dve.wait_ge(x_rstd, GROUPS * 1 + g + 1)
                            if due(g):
                                dve.wait_ge(f["ln_transposed"], g)
                            for t in range(GT):
                                i = dve_ln(dve, zs[:, t, :], GT * g + t)
                            i.then_inc(f["ln_ready"], 1)
                        if ok(s, 1):
                            kk, par = BLK0 * (g - 1) + k, (BLK0 * (s - 1) + k) % 2
                            dve.wait_ge(f["silu_ready"], kk + 1)
                            if due(kk - 1):
                                dve.wait_ge(f["block_added"], kk - 1)
                            if k < PAIRS:
                                dve.tensor_tensor(fa1[:, par, :], bank(2 + par), fsg[:, par, :], ALU.mult)\
                                   .then_inc(f["product_ready"], 1)
                                dve.wait_ge(f["product_ready"], PAIRS * (g - 1) + k + 1)
                                dve.tensor_tensor(fact[:, par, :], bank(6), fa1[:, par, :], ALU.mult)\
                                   .then_inc(f["act_ready"], 1)
                            else:
                                dve.tensor_tensor(fact[:, par, :], bank(2 + par), fsg[:, par, :], ALU.mult)\
                                   .then_inc(f["act_ready"], 1)
                        if ok(s, 0) and k == 3:
                            routing(0, s, g, 0)
                        if ok(s, 0) and k == 6:
                            routing(0, s, g, 1)
                        if ok(s, 2) and k == 1:
                            dve_y_stats(dve, 1, g - 2, s % 2)
                        if ok(s, 2) and k == 3:
                            dve_x_update(dve, 1, g - 2, s % 2)

            def moe1(b, ok):
                f = F[1]
                for s in range(2):
                    g = 2 * b + s
                    for k in range(BLK1):
                        if ok(s, 0) and k == 0:
                            dve.wait_ge(x_rstd, GROUPS * 3 + g + 1)
                            if due(g):
                                dve.wait_ge(f["ln_transposed"], g)
                            for t in range(GT):
                                i = dve_ln(dve, zs[:, t, :], GT * g + t)
                            i.then_inc(f["ln_ready"], 1)
                        if ok(s, 1):
                            e, c = divmod(k, NCH)
                            rows = CH[c][1]
                            kk, par = BLK1 * (g - 1) + k, k % 2
                            dve.wait_ge(f["silu_ready"], kk + 1)
                            if c == 0:
                                if due(E1 * (g - 1) + e - 1):
                                    dve.wait_ge(f["expert_ready"], E1 * (g - 1) + e - 1)
                            dve.tensor_tensor(fact1[0:rows, e % 2, c, :], bank(2 + par, GW, rows),
                                              fsg[0:rows, par, :], ALU.mult).then_inc(f["act_ready"], 1)
                            if k % NCH == NCH - 1 and e > 0:
                                combine(f, s, g - 1, e - 1)
                        if ok(s, 0) and k == 3:
                            routing(1, s, g, 0)
                        if ok(s, 0) and k == 6:
                            routing(1, s, g, 1)
                        if ok(s, 2) and k == 1:
                            dve_y_stats(dve, 3, g - 2, s % 2)
                        if ok(s, 2) and k == 4:
                            dve_x_update(dve, 3, g - 2, s % 2)
                    if ok(s, 1):
                        combine(f, s, g - 1, E1 - 1)

            def combine(f, s, g, e):
                par = (s - 1) % 2
                dve.wait_ge(f["expert_ready"], E1 * g + e + 1)
                if e > 0:
                    dve.wait_ge(f["expert_combined"], (E1 - 1) * g + e)
                for t in range(GT):
                    w = fcw[:, par, t, e:e + 1]
                    y = PS[:, 6 + e % 2, t * P:t * P + P]
                    if e == 0:
                        i = dve.tensor_scalar(ys[:, par, t, :], y, w, None, ALU.mult)
                    else:
                        i = dve.scalar_tensor_tensor(ys[:, par, t, :], y, w, ys[:, par, t, :], ALU.mult, ALU.add)
                i.then_inc(f["expert_combined"] if e < E1 - 1 else ys_ok, 1)

            def mamba_prep(s, g, n):
                if n == 0:
                    if due(g):
                        dve.wait_ge(MAM["ln_transposed"], g)
                    dve.wait_ge(MAM["scale_step"], 5 * g + 5)
                    for t in range(GT):
                        i = dve.tensor_scalar(zs[:, t, :], xt(GT * g + t), mean(GT * g + t), mr[:, 4, t:t + 1],
                                              ALU.subtract, ALU.mult)
                    i.then_inc(MAM["ln_ready"], 1)
                if n in (4, 5):
                    h = n - 4
                    dve.wait_ge(MAM["in_proj_copied"], 2 * g + h + 1)
                    for k in range(TAPS - 1):
                        dve.scalar_tensor_tensor(mu[:, h, :], mxin[:, h, k:k + GW], taps[:, h, k:k + 1], mu[:, h, :],
                                                 ALU.mult, ALU.add).then_inc(MAM["conv_step"], 1)
                        if k < TAPS - 2:
                            dve.wait_ge(MAM["conv_step"], 6 * g + 3 * h + k + 1)
                if n == 10:
                    dve.wait_ge(MAM["log_ready"], g + 1)
                    dve.scalar_tensor_tensor(mq[:, :, :], mw[:, :, :], -1.0, mex[:, :, :], ALU.add, ALU.subtract)\
                       .then_inc(MAM["correction_ready"], 1)
                if n == 11:
                    dve.scalar_tensor_tensor(mln[:, :, :], mxb[:, :, :], 0.0, mln[:, :, :], ALU.max, ALU.add)\
                       .then_inc(MAM["delta_partly_ready"], 1)
                    dve.wait_ge(MAM["delta_partly_ready"], g + 1)
                    dve.wait_ge(MAM["correction_ready"], g + 1)
                    if due(2 * N * (g - 1)):
                        dve.wait_ge(MAM["decay_ready"], 2 * N * (g - 1))
                    dve.tensor_tensor(mdl[:, s % 2], mln[:, :, :], mq[:, :, :], ALU.subtract).then_inc(MAM["delta_ready"], 1)

            def mamba_post(s, g, n):
                if n == 0:
                    dve.wait_ge(MAM["state_added"], N * g + N)
                    if due(g):
                        dve.wait_ge(MAM["gated_ready"], g)
                    for h in range(2):
                        i = dve.scalar_tensor_tensor(my[:, h, :], mxs[:, s % 2, h, :], wdd[:, h:h + 1], bank(h),
                                                     ALU.mult, ALU.add)
                    i.then_inc(MAM["y_ready"], 1)
                if n == 11:
                    dve.wait_ge(MAM["out_proj_ready"], g + 1)
                    for t in range(GT):
                        i = dve_ln(dve, mres[:, t, :], GT * g + t)
                    i.then_inc(MAM["residual_ready"], 1)
                    dve.wait_ge(MAM["residual_ready"], g + 1)
                    dve.tensor_tensor(ys[:, s % 2], bank_tiles(7), mres[:, :, :], ALU.add).then_inc(ys_ok, 1)
                if n == 12:
                    dve_y_stats(dve, 2, g, s % 2)
                if n == 14:
                    dve_x_update(dve, 2, g, s % 2)

            def mamba(b, ok):
                for s in range(2):
                    g = 2 * b + s
                    for n in range(N):
                        if ok(s, 1):
                            kk = N * (g - 1) + n
                            dve.wait_ge(MAM["delta_x_b_ready"], kk + 1)
                            if due(kk - 1):
                                dve.wait_ge(MAM["state_c_ready"], kk - 1)
                            if s == 1:
                                if due(N * b + n - 1):
                                    dve.wait_ge(MAM["state_kept"], N * b + n - 1)
                            elif n == 0:
                                dve.wait_ge(MAM["state_kept"], N * b)
                            for h in range(2):
                                dve.wait_ge(MAM["decay_ready"], 2 * kk + h + 1)
                                first = 0.0 if s == 1 else mhc[:, n, h:h + 1]
                                dve.tensor_tensor_scan(mh[:, n % 2, h, :], bank(4 + h), mdB[:, n % 2, h, :], first,
                                                       ALU.mult, ALU.add).then_inc(MAM["half_scanned"], 1)
                            dve.wait_ge(MAM["half_scanned"], 2 * kk + 2)
                            dve.wait_ge(MAM["c_spread"], kk + 1)
                            if due(kk - 1):
                                dve.wait_ge(MAM["state_added"], kk - 1)
                            dve.tensor_tensor(mP[:, n % 2], mh[:, n % 2],
                                              bank(2).rearrange("p (o t) -> p o t", o=1).to_broadcast([P, 2, GW]),
                                              ALU.mult).then_inc(MAM["state_c_ready"], 1)
                        if ok(s, 2):
                            mamba_post(s, g - 2, n)
                        if ok(s, 0):
                            mamba_prep(s, g, n)

            if stages > 1:
                stage_begins(dve, 1)
                const_wait(dve, 1)
                pipeline(dve, 2, 2, moe0)
            if stages > 2:
                stage_begins(dve, 2)
                const_wait(dve, 2)
                pipeline(dve, 2, 2, mamba)
            if stages > 3:
                stage_begins(dve, 3)
                pipeline(dve, 2, 2, moe1)

        @block.tensor
        def _(pe):
            mm = pe.matmul

            def attention(b, ok):
                for s in range(TB):
                    q = s % 2
                    if ok(s, 0):
                        i = TB * b + s
                        pe.wait_ge(ATT["ln_ready"], i + 1)
                        if due(i):
                            pe.wait_ge(ATT["lnT_copied"], i)
                        if due(i - 3):
                            pe.wait_ge(ATT["oT_copied"], i - 3)
                        pe.transpose(bank(0, P), az[:, q, :], ident[:, :]).then_inc(ATT["ln_transposed"], 1)
                    if ok(s, 2):
                        i = TB * b + s - 2
                        pe.wait_ge(ATT["kv_ready"], i + 1)
                        if due(i):
                            pe.wait_ge(ATT["product_ready"], i)
                        for c in range(2):
                            r = mm(bank(3 + c), tri[:, :], akv[:, q, 512 * c:512 * c + 512], start=True, stop=True)
                        r.then_inc(ATT["kv_cumulated"], 1)
                        if s != 2:
                            pe.wait_ge(ATT["qT_copied"], i + 1)
                            pe.wait_ge(ATT["state_masked"], i)
                            pe.wait_ge(ATT["o_ready"], i)
                            mm(bank(6, P), aqT[:, q, :], asm, start=True, stop=True)
                        if due(i):
                            pe.wait_ge(ATT["state_masked"], i)
                        mm(bank(5, P), aphi[:, q, P:2 * P], av[:, q, :], start=(s == 2), stop=True,
                           skip_group_check=True).then_inc(ATT["state_added"], 1)
                    if ok(s, 1):
                        i = TB * b + s - 1
                        pe.wait_ge(ATT["feature_ready"], i + 1)
                        pe.wait_ge(ATT["v_copied"], i + 1)
                        pe.transpose(bank(2, P), aphi[:, 1 - q, 0:P], ident[:, :]).then_inc(ATT["q_transposed"], 1)
                    if ok(s, 3):
                        i = TB * b + s - 3
                        pe.wait_ge(ATT["o_ready"], i + 1)
                        pe.wait_ge(ATT["lnT_copied"], i + 4 if not isinstance(b, int) or b < BATCHES else TILES)
                        pe.transpose(bank(0, P), ao[:, 1 - q, :], ident[:, :]).then_inc(ATT["o_transposed"], 1)
                    if ok(s, 0):
                        i = TB * b + s
                        pe.wait_ge(ATT["lnT_copied"], i + 1)
                        if due(i):
                            pe.wait_ge(ATT["feature_ready"], i)
                        mm(bank(1, 2 * P), ones[0:1, :], bqkv[0:1, 0:2 * P], start=True, stop=False)
                        mm(bank(1, 2 * P), azT[:, q, :], wqkv[:, 0:2 * P], start=False, stop=True).then_inc(ATT["qk_ready"], 1)
                        if due(i):
                            pe.wait_ge(ATT["qT_copied"], i)
                        mm(bank(2, P), ones[0:1, :], bqkv[0:1, 2 * P:3 * P], start=True, stop=False)
                        mm(bank(2, P), azT[:, q, :], wqkv[:, 2 * P:3 * P], start=False, stop=True).then_inc(ATT["v_ready"], 1)
                    if ok(s, 3):
                        i = TB * b + s - 3
                        t = (s - 3) % GT
                        pe.wait_ge(ATT["oT_copied"], i + 1)
                        if t == 0:
                            g = (TB // GT) * b + (s - 3) // GT
                            if due(g):
                                pe.wait_ge(ys_ok, g)
                        o = PS[:, 7, t * P:t * P + P]
                        mm(o, ones[0:1, :], bo[0:1, :], start=True, stop=False)
                        mm(o, aoT[:, 1 - q, :], wo[:, :], start=False, stop=True).then_inc(ATT["y_ready"], 1)
            const_wait(pe, 0)
            pe.wait_ge(pool_const, 1)
            pipeline(pe, TB, 1, attention)

            def transpose_zs(f, g, k):
                pe.wait_ge(f["ln_ready"], g + 1)
                if due(g):
                    pe.wait_ge(f["lnT_copied"], g)
                for t in range(GT):
                    r = pe.transpose(PS[:, k, t * P:t * P + P], zs[:, t, :], ident[:, :])
                r.then_inc(f["ln_transposed"], 1)

            def moe_prep(m, s, g, k):
                f = F[m]
                if k == 0:
                    transpose_zs(f, g, 0)
                if k == 2:
                    E, w = ((E0, wg0), (E1, wg1))[m]
                    pe.wait_ge(f["lnT_copied"], g + 1)
                    if due(g):
                        pe.wait_ge(f["logits_shifted"], g)
                    for t in range(GT):
                        r = mm(PS[:, 1, t * E:t * E + E], fzT[:, s % 2, t * P:t * P + P], w[:, :], start=True, stop=True)
                    r.then_inc(f["logits_ready"], 1)

            def moe0(b, ok):
                f = F[0]

                def down(s, g, k):
                    kk, par = BLK0 * g + k, (BLK0 * (s - 1) + k) % 2
                    pe.wait_ge(f["act_ready"], kk + 1)
                    if k == 0:
                        pe.wait_ge(ys_ok, GROUPS + g)
                    for t in range(GT):
                        r = mm(PS[:, 7, t * P:t * P + P], fact[:, par, t * P:t * P + P], w2[:, k, :],
                               start=(k == 0 and t == 0), stop=(k == BLK0 - 1), skip_group_check=True)
                    r.then_inc(f["block_added"], 1)
                for s in range(2):
                    g = 2 * b + s
                    for k in range(BLK0):
                        if ok(s, 1):
                            kk, par = BLK0 * (g - 1) + k, (BLK0 * (s - 1) + k) % 2
                            z = fzT[:, (s - 1) % 2, :]
                            if due(kk - 1):
                                pe.wait_ge(f["act_ready"], kk - 1)
                            mm(bank(2 + par), w1u[:, k, :], z, start=True, stop=True)
                            if due(kk - 1):
                                pe.wait_ge(f["silu_ready"], kk - 1)
                            r = mm(bank(4 + par), w1g[:, k, :], z, start=True, stop=True)
                            if k < PAIRS:
                                pe.wait_ge(f["weights_widened"], g)
                                if due(kk):
                                    pe.wait_ge(f["act_ready"], kk)
                                for t in range(GT):
                                    r = pe.transpose(PS[:, 6, t * P:t * P + P],
                                                     fwide[:, (s - 1) % 2, t, P * k:P * k + P], ident[:, :])
                            r.then_inc(f["up_gate_ready"], 1)
                            if k > 0:
                                down(s, g - 1, k - 1)
                        if ok(s, 0):
                            moe_prep(0, s, g, k)
                    if ok(s, 1):
                        down(s, g - 1, BLK0 - 1)

            def moe1(b, ok):
                f = F[1]

                def down(g, e):
                    ee = E1 * g + e
                    pe.wait_ge(f["act_ready"], NCH * ee + NCH)
                    if e >= 2:
                        pe.wait_ge(f["expert_combined"], (E1 - 1) * g + e - 1)
                    elif e == 1:
                        pe.wait_ge(ys_ok, GROUPS * 3 + g)
                    else:
                        if due((E1 - 1) * g):
                            pe.wait_ge(f["expert_combined"], (E1 - 1) * g)
                    for t in range(GT):
                        for c, (_, rows) in enumerate(CH):
                            r = mm(PS[:, 6 + e % 2, t * P:t * P + P], fact1[0:rows, e % 2, c, t * P:t * P + P],
                                   wc[0:rows, e, c, :], start=(c == 0), stop=(c == NCH - 1))
                    r.then_inc(f["expert_ready"], 1)
                for s in range(2):
                    g = 2 * b + s
                    for k in range(BLK1):
                        if ok(s, 1):
                            e, c = divmod(k, NCH)
                            off, rows = CH[c]
                            kk, par = BLK1 * (g - 1) + k, k % 2
                            z = fzT[:, (s - 1) % 2, :]
                            if due(kk - 1):
                                pe.wait_ge(f["act_ready"], kk - 1)
                            mm(bank(2 + par, GW, rows), wb[:, e * H1 + off:e * H1 + off + rows], z, start=True, stop=True)
                            mm(bank(4 + par, GW, rows), wa[:, e * H1 + off:e * H1 + off + rows], z, start=True, stop=True)\
                                .then_inc(f["up_gate_ready"], 1)
                            if c == 0 and e > 0:
                                down(g - 1, e - 1)
                        if ok(s, 0):
                            moe_prep(1, s, g, k)
                    if ok(s, 1):
                        down(g - 1, E1 - 1)

            def column(k, par, j):
                for t in range(GT):
                    r = pe.transpose(PS[:, k, t * P:t * P + P], mbc[:, par, t, j:j + 1].to_broadcast([P, P]), ident[:, :])
                return r

            def mamba_B(g, par, n):
                kk = N * g + n
                if n == 0:
                    pe.wait_ge(MAM["bc_copied"], g + 1)
                if due(kk):
                    pe.wait_ge(MAM["b_copied"], kk)
                column(3, par, n).then_inc(MAM["b_spread"], 1)

            def add_state(g, n):
                kk = N * g + n
                pe.wait_ge(MAM["state_c_ready"], kk + 1)
                if n == 0:
                    if due(g):
                        pe.wait_ge(MAM["y_ready"], g)
                for h in range(2):
                    r = mm(bank(h), ident[:, :], mP[:, n % 2, h, :], start=(n == 0), stop=(n == N - 1))
                r.then_inc(MAM["state_added"], 1)

            def mamba_prep(s, g, n):
                par = s % 2
                if n == 1:
                    if due(2 * g):
                        pe.wait_ge(MAM["d2_copied"], 2 * g)
                    transpose_zs(MAM, g, 6)
                if n in (2, 3):
                    h = n - 2
                    pe.wait_ge(MAM["lnT_copied"], g + 1)
                    if h == 0:
                        pe.wait_ge(ys_ok, GROUPS * 2 + g - 2)
                    mm(bank(7 - h), win[:, h * P:h * P + P], mxn, start=True, stop=True).then_inc(MAM["in_proj_ready"], 1)
                if n == 4:
                    for h in range(2):
                        pe.wait_ge(MAM["in_proj_copied"], 2 * g + h + 1)
                        mm(bank(7 - h), wskip[:, h * P:h * P + P], mxn, start=True, stop=True).then_inc(MAM["skip_ready"], 1)
                if n == 7:
                    pe.wait_ge(MAM["x_silu_ready"], g + 1)
                    pe.wait_ge(MAM["skip_silu_ready"], 2 * g + 2)
                    for h in range(2):
                        r = mm(bank(7, GW, DD), wd1[:, h, :], mxs[:, par, h, :], start=(h == 0), stop=(h == 1))
                    r.then_inc(MAM["d1_ready"], 1)
                    for t in range(GT):
                        for h in range(2):
                            r = mm(PS[:, 6, t * 2 * N:(t + 1) * 2 * N], mxs[:, par, h, t * P:t * P + P], wbc[:, h, :],
                                   start=(h == 0), stop=(h == 1))
                    r.then_inc(MAM["bc_ready"], 1)
                if n == 8:
                    pe.wait_ge(MAM["d1_copied"], g + 1)
                    pe.wait_ge(MAM["bc_copied"], g + 1)
                    for h in range(2):
                        mm(bank(7 - h), wd2[:, h * P:h * P + P], md1[0:DD, :], start=True, stop=True).then_inc(MAM["d2_ready"], 1)

            def mamba_post(s, g, n, prep):
                if n == 10:
                    pe.wait_ge(MAM["gated_ready"], g + 1)
                    pe.wait_ge(MAM["d2_copied"], 2 * (g + 3) if prep else 2 * GROUPS)
                    for t in range(GT):
                        for h in range(2):
                            r = mm(PS[:, 7, t * P:t * P + P], myg[:, h, t * P:t * P + P], wout[:, h, :],
                                   start=(h == 0), stop=(h == 1))
                    r.then_inc(MAM["out_proj_ready"], 1)

            def mamba(b, ok):
                for s in range(2):
                    g = 2 * b + s
                    for n in range(N):
                        if ok(s, 1):
                            kk = N * (g - 1) + n
                            if n < N - 1:
                                mamba_B(g - 1, (s - 1) % 2, n + 1)
                            if due(kk):
                                pe.wait_ge(MAM["state_c_ready"], kk)
                            column(2, (s - 1) % 2, N + n).then_inc(MAM["c_spread"], 1)
                            if n > 0:
                                add_state(g - 1, n - 1)
                        if ok(s, 0):
                            mamba_prep(s, g, n)
                        if ok(s, 2):
                            mamba_post(s, g - 2, n, ok(s, 0))
                        if ok(s, 0) and n == N - 1:
                            mamba_B(g, s % 2, 0)
                    if ok(s, 1):
                        add_state(g - 1, N - 1)

            if stages > 1:
                stage_begins(pe, 1)
                const_wait(pe, 1)
                pipeline(pe, 2, 2, moe0)
            if stages > 2:
                stage_begins(pe, 2)
                pipeline(pe, 2, 2, mamba)
            if stages > 3:
                stage_begins(pe, 3)
                const_wait(pe, 3)
                pipeline(pe, 2, 2, moe1)


STAGES = 4


def kernel(**inputs):
    import numpy as np
    import concourse.bacc as bacc
    from concourse import mybir as mb
    from concourse.bass_utils import run_bass_kernel_spmd

    a = {k: np.asarray(v) for k, v in inputs.items()}
    c = np.ascontiguousarray

    def halves(w):
        return c(w.reshape(2, P, -1).transpose(1, 0, 2))

    def blocks(w1, shared):
        pairs = w1.reshape(PAIRS, 2, P, H0).transpose(2, 0, 1, 3).reshape(P, PAIRS, P)
        return c(np.concatenate([pairs, shared[:, None, :]], axis=1))

    w1, ws1 = a["L0_ffn_W1"], a["L0_ffn_Ws1"]
    w3 = a["L1_ffn_w3"].transpose(2, 0, 1)
    wc = np.zeros((P, E1, NCH, P), np.float32)
    for k, (off, rows) in enumerate(CH):
        wc[:rows, :, k, :] = w3[off:off + rows]
    arrays = {
        "x": c(a["L0_attn_x"]),
        "ident": np.eye(P, dtype=np.float32),
        "tri": np.triu(np.ones((P, P), np.float32)),
        "heads": np.kron(np.eye(HEADS, dtype=np.float32), np.ones((HD, HD), np.float32)),
        "rev": c(np.broadcast_to(np.arange(E0, 0, -1, dtype=np.float32), (P, E0))),
        "wqkv": c(np.concatenate([a["L0_attn_Wq"].T, a["L0_attn_Wk"].T, a["L0_attn_Wv"].T], axis=1)),
        "bqkv": c(np.concatenate([a["L0_attn_bq"], a["L0_attn_bk"], a["L0_attn_bv"]])[None, :]),
        "wo": c(a["L0_attn_Wo"].T),
        "bo": c(a["L0_attn_bo"][None, :]),
        "wg0": c(a["L0_ffn_Wg"].T),
        "w1u": blocks(c(w1[:, :, :H0]), ws1[:, :P]),
        "w1g": blocks(c(w1[:, :, H0:]), ws1[:, P:]),
        "w2": c(np.concatenate([a["L0_ffn_W2"].reshape(PAIRS, P, P), a["L0_ffn_Ws2"][None]], axis=0).transpose(1, 0, 2)),
        "nw": c(a["L1_attn_norm_w"][:, None]),
        "wskip": c(a["L1_attn_skip_w"].T),
        "win": c(a["L1_attn_in_w"].T),
        "taps": halves(a["L1_attn_conv_w"][:, 0, :]),
        "cb": c(a["L1_attn_conv_b"].reshape(2, P).T),
        "wd1": halves(a["L1_attn_Wd1"].T),
        "wd2": c(a["L1_attn_Wd2_w"].T),
        "bd2": c(a["L1_attn_Wd2_b"].reshape(2, P).T),
        "wbc": halves(np.concatenate([a["L1_attn_WB"].T, a["L1_attn_WC"].T], axis=1)),
        "alog": halves(a["L1_attn_A_log"]),
        "wdd": c(a["L1_attn_W_D"].reshape(2, P).T),
        "wout": halves(a["L1_attn_out_w"].T),
        "wg1": c(a["L1_ffn_gate_w"].T),
        "wa": c(a["L1_ffn_w1"].transpose(2, 0, 1).reshape(P, E1 * H1)),
        "wb": c(a["L1_ffn_w2"].transpose(2, 0, 1).reshape(P, E1 * H1)),
        "wc": wc,
    }
    nc = bacc.Bacc("TRN2", target_bir_lowering=False, num_devices=1)
    aps = {n: nc.dram_tensor("in_" + n, v.shape, mb.dt.from_np(v.dtype), kind="ExternalInput").ap()
           for n, v in arrays.items()}
    out = nc.dram_tensor("out_x", a["L0_attn_x"].shape, mb.dt.float32, kind="ExternalOutput").ap()
    program(nc, aps, out, STAGES)
    r = run_bass_kernel_spmd(nc, [{"in_" + n: v for n, v in arrays.items()}], core_ids=[0])
    return r.results[0]["out_x"]
```

```python
from contextlib import ExitStack

import concourse.bass as bass
from concourse import mybir

ALU = mybir.AluOpType
ACT = mybir.ActivationFunctionType
F32 = mybir.dt.float32
BF16 = mybir.dt.bfloat16
F32R = mybir.dt.float32r
AX_X = mybir.AxisListType.X

P = 128
TILES = 32
BATCHES = 4
TB = 8
GT = 4
GROUPS = 8
GW = GT * P
EPS = 1e-5
HEADS, HD = 16, 8
E0, H0 = 16, 64
PAIRS = E0 // 2
BLK0 = PAIRS + 1
E1, H1 = 8, 341
NCH = 3
BLK1 = E1 * NCH
BLKS, EXPERTS, ROWS = (BLK0, BLK1), (E0, E1), (PAIRS, E1)
ROUTING = 20
PIECE = 3
N = 16
DD = 64
TAPS = 4
ARENA = 30794


def due(count):
    return not isinstance(count, int) or count > 0


def pipeline(eng, slots, peel, emit, longest=2):
    for b in range(peel):
        emit(b, lambda s, lag, b=b: b * slots + s >= lag)
    with eng.Fori(peel, BATCHES) as b:
        emit(b, lambda s, lag: True)
    emit(BATCHES, lambda s, lag: s < lag)
    if longest > slots:
        emit(BATCHES + 1, lambda s, lag: s + slots < lag)


def program(nc, A, out, stages=4):
    with ExitStack() as ctx:
        def sb(name, shape, dt=F32):
            return ctx.enter_context(nc.sbuf_tensor(name, shape, dt))

        def sem(name):
            return ctx.enter_context(nc.semaphore(name))

        X = sb("X", [P, TILES, P])
        MV = sb("MV", [P, TILES, 2])
        RS = sb("RS", [P, TILES])
        ident = sb("ident", [P, P])
        tri = sb("tri", [P, P])
        heads = sb("heads", [P, P])
        rev = sb("rev", [P, E0])
        ones = sb("ones", [1, P])
        mhalf = sb("mhalf", [P, GT])
        wqkv = sb("wqkv", [P, 3 * P])
        bqkv = sb("bqkv", [1, 3 * P])
        wo = sb("wo", [P, P])
        bo = sb("bo", [1, P])
        wg0 = sb("wg0", [P, E0])
        nw = sb("nw", [P, 1])
        wskip = sb("wskip", [P, 2 * P])
        win = sb("win", [P, 2 * P])
        taps = sb("taps", [P, 2, TAPS])
        cb = sb("cb", [P, 2])
        wd1 = sb("wd1", [P, 2, DD])
        wd2 = sb("wd2", [DD, 2 * P])
        bd2 = sb("bd2", [P, 2])
        wbc = sb("wbc", [P, 2, P])
        pick = sb("pick", [P, 2 * N])
        pickb = sb("pickb", [P, 2 * N], BF16)
        alog = sb("alog", [P, 2, N])
        aneg = sb("aneg", [P, 2, N])
        wdd = sb("wdd", [P, 2])
        diag = sb("diag", [P, 2, P])
        wout = sb("wout", [P, 2, P])
        wg1 = sb("wg1", [P, E1])
        pickm = sb("pickm", [P, E0])
        pickmb = sb("pickmb", [P, E0], BF16)
        identb = sb("identb", [P, P], BF16)

        ys = sb("ys", [P, 2, GT, P])
        tmp = sb("tmp", [P, GT, P])
        bny = sb("bny", [P, GT, 6])
        mvy = sb("mvy", [P, GT, 2])
        rsy = sb("rsy", [P, GT])
        vy = sb("vy", [P, GT])
        vx = sb("vx", [P, GT])
        bnx = sb("bnx", [P, GT, 6])
        mvx = sb("mvx", [P, GT, 2])
        eps = sb("eps", [P, GT])
        one = sb("one", [P, 2])
        mneg = sb("mneg", [P, 1])
        mr = sb("mr", [P, 3, TILES])
        mt = sb("mt", [P, 5, GT])
        carried = sb("carried", [P, 16])
        zs = sb("zs", [P, GT, P])

        def in_place(*tensors):
            with ExitStack() as scope:
                return [scope.enter_context(nc.sbuf_tensor(*t)) for t in tensors]

        wm0, = in_place(("wm0", [P, BLK0, 3, P], F32))
        wm1 = sb("wm1", [P, BLK1, 3, P])
        wm = (wm0, wm1)
        arena, = in_place(("arena", [P, ARENA], F32))

        def moe_buffers(m):
            names = dict(
                w=([P, 2, BLKS[m], 3, P], F32R),
                z=([P, 2, 2, GW], F32R),
                a=([P, 3, 2, GW], F32R),
                zf=([P, GW], F32),
                silu=([P, 2, GW], F32), product=([P, 2, GW], F32), weighted=([P, 2, GW], F32),
                cwB=([P, 2, GW], F32),
                yT=([P, GW], F32),
                cw=([P, GT, E0], F32), rest=([P, GT, E0], F32),
                cwp=([P, GT, 96], BF16),
                cwT=([P, 2, GW], BF16),
                m=([P, GT], F32), l=([P, GT, E0], F32), ex=([P, GT, E0], F32), p=([P, GT, E0], F32), s=([P, GT], F32),
                rs=([P, GT], F32), eq=([P, GT, E0], F32), oh=([P, 2, GT, E0], F32), l2=([P, GT, E0], F32))
            if m == 0:
                names["wide"] = ([P, E0, H0], BF16)
            return dict(zip(names, in_place(*((f"m{m}_{n}", *v) for n, v in names.items()))))
        BUF = (moe_buffers(0), moe_buffers(1))
        used = [0]

        def carve(*shape):
            n = 1
            for d in shape:
                n *= d
            ap = arena[:, used[0]:used[0] + n]
            used[0] += n
            assert used[0] <= ARENA, used[0]
            names = "abcde"[:len(shape)]
            if len(shape) == 1:
                return ap
            return ap.rearrange("p (" + " ".join(names) + ") -> p " + " ".join(names),
                                **{names[k]: shape[k] for k in range(1, len(shape))})

        az = carve(2, P)
        azT = carve(2, P)
        amn = carve(2, 2 * P)
        aex = carve(2, 2 * P)
        aphi = carve(2, 2 * P)
        av = carve(2, P)
        akv = carve(2, HEADS * HD * HD)
        aqT = carve(2, P)
        aprod = carve(HEADS * HD * HD)
        ared = carve(P)
        ao = carve(2, P)
        aoT = carve(2, P)
        asm = carve(P)
        used[0] = 0
        mxn = carve(GW)
        mxin = carve(2, TAPS - 1 + GW)
        mu = carve(2, GW)
        mxs = carve(2, 2, GW)
        msk = carve(2, 2, GW)
        md1 = carve(GW)
        mxb = carve(2, GW)
        mab = carve(2, GW)
        mw = carve(2, GW)
        mq = mw
        mdl = carve(2, 2, GW)
        mdx = carve(2, 2, GW)
        mbc = carve(GW)
        mparts = carve(GW).bitcast(BF16).rearrange("p (q t) -> p q t", q=2)
        mBs = carve(4, GW)
        mdB = carve(4, 2, GW)
        mdec = carve(4, 2, GW)
        mh = carve(2, 2, GW)
        mhc = carve(N, 2)
        mP = carve(2, 2, GW)
        myg = carve(2, GW)

        PS = ctx.enter_context(nc.psum_tensor("PS", [P, 8, 512], F32))

        def bank(k, n=512, p=P):
            return PS[0:p, k, 0:n]

        def bank_tiles(k, w=P):
            return PS[:, k, 0:GT * w].rearrange("p (t w) -> p t w", w=w)

        s_x = [sem(f"s_x{b}") for b in range(BATCHES)]
        s_c = [sem(f"s_c{i}") for i in range(4)]
        s_out = sem("s_out")
        x_stats, x_rstd, vx_ok = sem("x_stats"), sem("x_rstd"), sem("vx_ok")
        ys_ok, y_stats, y_rstd, vy_ok = sem("ys_ok"), sem("y_stats"), sem("y_rstd"), sem("vy_ok")
        ep = sem("ep")
        pool_const = sem("pool_const")
        ATT = {n: sem(f"a_{n}") for n in (
            "ln_ready", "ln_transposed", "lnT_copied", "qk_ready", "v_ready", "x_read", "min_ready", "exp_ready", "v_copied",
            "feature_ready", "kv_ready", "q_transposed", "qT_copied", "kv_cumulated", "state_added",
            "product_ready", "product_summed", "state_masked", "o_ready", "o_transposed", "oT_copied", "y_ready")}
        F = [{n: sem(f"f{m}_{n}") for n in (
            "high_weights_ready", "low_weights_ready", "ln_ready", "ln_transposed", "lnT_copied", "low_ln_ready",
            "logits_ready", "logits_shifted", "exp_ready", "routing_step", "maximum_ready", "weights_ready",
            "weights_transposed",
            "weights_copied", "row_ready", "row_copied", "up_gate_ready", "silu_ready", "product_ready",
            "weighted_ready", "high_ready", "low_ready", "block_added", "yT_copied", "y_transposed",
            "constants_ready")} for m in range(2)]
        MAM = {n: sem(f"m_{n}") for n in (
            "scale_step", "ln_ready", "ln_transposed", "lnT_copied", "in_proj_ready", "in_proj_copied",
            "carry_ready", "conv_step", "skip_ready", "skip_silu_ready", "x_silu_ready", "d1_ready", "d1_copied",
            "bc_ready", "bc_copied", "bc_rest_ready", "bc_part_ready", "d2_ready", "d2_copied", "abs_ready", "exp_ready", "one_plus_exp_ready",
            "log_ready", "correction_ready", "delta_partly_ready", "delta_ready", "delta_x_ready", "b_spread",
            "b_copied", "c_spread", "delta_x_b_ready", "decay_ready", "half_scanned", "state_c_ready",
            "state_added", "gated_ready", "diagonal_ready", "out_proj_ready", "residual_ready", "a_ready", "state_kept")}
        EPN = 4

        def group(T, g):
            return T[:, bass.ds(GT * g, GT)]

        def xt(i):
            return X[:, bass.ds(i, 1), :].rearrange("p a d -> p (a d)")

        def mean(i):
            return MV[:, bass.ds(i, 1), 0:1].rearrange("p a c -> p (a c)")

        def wide(ap, n):
            return ap.rearrange("p (t o) -> p t o", o=1).to_broadcast([P, GT, n])

        carriers = [0, 0]

        def pool_carrier():
            k = carriers[0] = (carriers[0] + 1) % 8
            nc.gpsimd.tensor_tensor(carried[:, k:k + 1], one[:, 0:1], one[:, 0:1], ALU.mult)

        def dve_carrier():
            k = carriers[1] = (carriers[1] + 1) % 8
            nc.vector.memset(carried[:, 8 + k:9 + k], 0.0)

        def pool_x_rstd(pool, st, g):
            n = GROUPS * st + g + 1
            pool.wait_ge(x_stats, n)
            pool.tensor_tensor(vx[:, :], mvx[:, :, 1], eps[:, :], ALU.add).then_inc(vx_ok, 1)
            pool.tensor_copy(group(MV, g), mvx[:, :, :])
            pool.wait_ge(vx_ok, n)
            pool_carrier()
            pool.tensor_tensor(group(RS, g), vx[:, :], mhalf[:, :], ALU.pow).then_inc(x_rstd, 1)

        def pool_y_rstd(pool, st, g):
            n = GROUPS * st + g + 1
            pool.wait_ge(y_stats, n)
            pool.tensor_tensor(vy[:, :], mvy[:, :, 1], eps[:, :], ALU.add).then_inc(vy_ok, 1)
            pool.wait_ge(vy_ok, n)
            pool.tensor_tensor(rsy[:, :], vy[:, :], mhalf[:, :], ALU.pow).then_inc(y_rstd, 1)

        def ep_count(st, g, c):
            per = EPN if st < stages - 1 else EPN - 1
            return EPN * GROUPS * st + per * g + c

        def stage_begins(eng, st):
            if st:
                eng.wait_ge(ys_ok, GROUPS * st)

        def dve_y_stats(dve, st, g, par):
            dve.wait_ge(ys_ok, GROUPS * st + g + 1)
            if due(GROUPS * st + g):
                dve.wait_ge(y_stats, GROUPS * st + g)
            for t in range(GT):
                i = dve.bn_stats(bny[:, t, :], ys[:, par, t, :])
            i.then_inc(ep, 1)
            dve.wait_ge(ep, ep_count(st, g, 1))
            dve_carrier()
            for t in range(GT):
                i = dve.bn_aggr(mvy[:, t, :], bny[:, t, :])
            i.then_inc(y_stats, 1)

        def dve_x_update(dve, st, g, par):
            dve.wait_ge(y_rstd, GROUPS * st + g + 1)
            for t in range(GT):
                i = dve.tensor_scalar(tmp[:, t, :], ys[:, par, t, :], mvy[:, t, 0:1], rsy[:, t:t + 1],
                                      ALU.subtract, ALU.mult)
            i.then_inc(ep, 1)
            dve.wait_ge(ep, ep_count(st, g, 2))
            dve.tensor_tensor(group(X, g), group(X, g), tmp[:, :, :], ALU.add).then_inc(ep, 1)

        def dve_new_stats(dve, st, g):
            if st < stages - 1:
                dve_x_stats(dve, g, ep, ep_count(st, g, 4), GROUPS * (st + 1) + g, (ep, ep_count(st, g, 3)))

        def dve_x_stats(dve, g, s, n, rstd_before, *before):
            if due(rstd_before):
                dve.wait_ge(x_stats, rstd_before)
            for before_sem, before_n in before:
                dve.wait_ge(before_sem, before_n)
            dve_carrier()
            for t in range(GT):
                i = dve.bn_stats(bnx[:, t, :], xt(GT * g + t))
            i.then_inc(s, 1)
            dve.wait_ge(s, n)
            if due(rstd_before):
                dve.wait_ge(x_rstd, rstd_before)
            dve_carrier()
            for t in range(GT):
                i = dve.bn_aggr(mvx[:, t, :], bnx[:, t, :])
            i.then_inc(x_stats, 1)

        def dve_ln(dve, dst, i):
            return dve.tensor_scalar(dst, xt(i), mean(i), RS[:, bass.ds(i, 1)], ALU.subtract, ALU.mult)

        consts = (
            (("ident", ident), ("wqkv", wqkv), ("bqkv", bqkv), ("tri", tri), ("heads", heads), ("wo", wo), ("bo", bo)),
            (("rev", rev), ("wg0", wg0), ("pickm", pickm), ("wm0", wm0)),
            (("nw", nw), ("wskip", wskip), ("win", win), ("cb", cb), ("wd2", wd2), ("bd2", bd2), ("wdd", wdd),
             ("taps", taps), ("wd1", wd1), ("wbc", wbc), ("pick", pick), ("alog", alog), ("wout", wout)),
            (("wg1", wg1), ("wm1", wm1)),
        )

        def const_wait(eng, st):
            eng.wait_ge(s_c[st], 16 * len(consts[st]))

        def full(t):
            return t[tuple(slice(None) for _ in t.shape)]

        block = ctx.enter_context(nc.Block())

        @block.sync
        def _(sp):
            for b in range(BATCHES):
                sp.dma_start(X[:, TB * b:TB * b + TB, :], A["x"][b].rearrange("(t p) d -> p t d", p=P)).then_inc(s_x[b], 16)
                if b == 0:
                    for name, dst in consts[0]:
                        sp.dma_start(full(dst), A[name]).then_inc(s_c[0], 16)
            for st in range(1, 4):
                if st == 3:
                    sp.wait_ge(F[0]["low_weights_ready"], BLK0 // PIECE)
                for name, dst in consts[st]:
                    sp.dma_start(full(dst), A[name]).then_inc(s_c[st], 16)
            for g in range(GROUPS):
                sp.wait_ge(ep, ep_count(stages - 1, g, 3))
                sp.dma_start(out.rearrange("b (t p) d -> p (b t) d", p=P)[:, GT * g:GT * g + GT, :],
                             X[:, GT * g:GT * g + GT, :]).then_inc(s_out, 16)
            sp.wait_ge(s_out, 16 * GROUPS)

        @block.gpsimd
        def _(pool):
            pool.memset(ones[:, :], 1.0)
            pool.memset(eps[:, :], EPS)
            pool.memset(one[:, :], 1.0)
            pool.memset(mneg[:, :], -1.0)
            pool.memset(mhalf[:, :], -0.5).then_inc(pool_const, 1)
            pool.wait_ge(pool_const, 1)
            for g in range(2):
                pool_x_rstd(pool, 0, g)

            def attention(b, ok):
                for s in range(TB):
                    if ok(s, 1):
                        i, q = TB * b + s - 1, (s - 1) % 2
                        pool.wait_ge(ATT["feature_ready"], i + 1)
                        pool.wait_ge(ATT["v_copied"], i + 1)
                        if due(i - 1):
                            pool.wait_ge(ATT["kv_cumulated"], i - 1)
                        k4 = aphi[:, q, P:2 * P].rearrange("p (h o d) -> p h o d", h=HEADS, o=1)
                        v4 = av[:, q, :].rearrange("p (h e o) -> p h e o", h=HEADS, o=1)
                        shape = [P, HEADS, HD, HD]
                        pool.tensor_tensor(akv[:, q, :].rearrange("p (h e d) -> p h e d", e=HD, d=HD),
                                           k4.to_broadcast(shape), v4.to_broadcast(shape), ALU.mult).then_inc(ATT["kv_ready"], 1)
                    if ok(s, 4) and (s - 4) % GT == GT - 1:
                        g = (TB // GT) * b + (s - 4 - (GT - 1)) // GT
                        pool_y_rstd(pool, 0, g)
                    if ok(s, 6) and (s - 6) % GT == GT - 1 and stages > 1:
                        pool_x_rstd(pool, 1, (TB // GT) * b + (s - 6 - (GT - 1)) // GT)
                    if isinstance(b, int) and b == 0 and s < GROUPS - 2:
                        pool_x_rstd(pool, 0, s + 2)
            pipeline(pool, TB, 1, attention)

            def mamba_scales(g):
                step, rs, out3 = MAM["scale_step"], group(RS, g), [group(mr[:, i], g) for i in range(3)]
                neg = mneg[:, 0:1].to_broadcast([P, GT])
                pool.wait_ge(x_rstd, GROUPS * 2 + g + 1)
                if due(8 * g):
                    pool.wait_ge(step, 8 * g)
                pool_carrier()
                pool.tensor_tensor(mt[:, 0], rs, rs, ALU.mult).then_inc(step, 1)
                pool.wait_ge(step, 8 * g + 1)
                pool_carrier()
                pool.tensor_tensor(mt[:, 1], mt[:, 0], group(MV, g)[:, :, 1], ALU.mult).then_inc(step, 1)
                pool.wait_ge(step, 8 * g + 2)
                pool.tensor_tensor(mt[:, 2], mt[:, 1], eps[:, :], ALU.add).then_inc(step, 1)
                pool.wait_ge(step, 8 * g + 3)
                pool.tensor_tensor(mt[:, 3], mt[:, 2], mhalf[:, :], ALU.pow).then_inc(step, 1)
                pool.wait_ge(step, 8 * g + 4)
                pool_carrier()
                pool.tensor_tensor(out3[0], mt[:, 3], rs, ALU.mult).then_inc(step, 1)
                pool.tensor_tensor(mt[:, 4], group(MV, g)[:, :, 0], neg, ALU.mult).then_inc(step, 1)
                pool.wait_ge(step, 8 * g + 6)
                pool_carrier()
                pool.tensor_tensor(out3[1], mt[:, 4], out3[0], ALU.mult).then_inc(step, 1)
                pool.tensor_tensor(out3[2], mt[:, 4], rs, ALU.mult).then_inc(step, 1)

            def moe(st, m):
                f, B, buf = F[m], BLKS[m], BUF[m]

                def emit(b, ok):
                    for s in range(2):
                        g = 2 * b + s
                        for k in range(B):
                            if ok(s, 1):
                                kk, par = B * (g - 1) + k, (B * (s - 1) + k) % 2
                                pool.wait_ge(f["product_ready"], kk + 1)
                                if due(kk - 1):
                                    pool.wait_ge(f["low_ready"], kk - 1)
                                j = k if m == 0 else k // NCH
                                if j < ROWS[m]:
                                    pool.wait_ge(f["row_copied"], ROWS[m] * (g - 1) + j + 1)
                                    w = buf["cwB"][:, j % 2, :]
                                else:
                                    w = one[:, 0:1].to_broadcast([P, GW])
                                pool.tensor_tensor(buf["weighted"][:, par, :], buf["product"][:, par, :], w,
                                                   ALU.mult).then_inc(f["weighted_ready"], 1)
                            if ok(s, 0) and k == 3:
                                pool.wait_ge(f["lnT_copied"], g + 1)
                                if due(B * (g - 1)):
                                    pool.wait_ge(f["up_gate_ready"], B * (g - 1))
                                pool.tensor_tensor(buf["z"][:, s % 2, 1, :], buf["zf"][:, :],
                                                   buf["z"][:, s % 2, 0, :].bitcast(F32), ALU.subtract).then_inc(f["low_ln_ready"], 1)
                            if ok(s, 2) and k == 6:
                                pool_y_rstd(pool, st, g - 2)
                            if ok(s, 3) and k == 1 and st < stages - 1:
                                pool_x_rstd(pool, st + 1, g - 3)
                            if ok(s, 3) and k == 3 and st == 1 and stages > 2:
                                mamba_scales(g - 3)
                stage_begins(pool, st)
                pipeline(pool, 2, 2, emit, longest=3)

            def mamba_prep(s, g, n):
                if n == 1:
                    if due(6 * g):
                        pool.wait_ge(MAM["conv_step"], 6 * g)
                    pool_carrier()
                    if s == 0:
                        pool.memset(mxin[:, :, 0:TAPS - 1], 0.0).then_inc(MAM["carry_ready"], 1)
                    else:
                        pool.tensor_copy(mxin[:, :, 0:TAPS - 1], mxin[:, :, GW:GW + TAPS - 1]).then_inc(MAM["carry_ready"], 1)
                if n in (9, 11):
                    pool.wait_ge(MAM["bc_copied"], g + 1)
                    if n == 11:
                        pool.wait_ge(MAM["bc_part_ready"], 2 * g + 1)
                    pool.tensor_tensor(mbc[:, :], mbc[:, :], mparts[:, s % 2, :], ALU.subtract)\
                       .then_inc(MAM["bc_rest_ready"], 1)
                if n == 13:
                    pool.wait_ge(MAM["delta_ready"], g + 1)
                    pool.tensor_tensor(mdx[:, s % 2], mdl[:, s % 2], mxs[:, s % 2], ALU.mult).then_inc(MAM["delta_x_ready"], 1)

            def pool_dB(g, par, n):
                kk = N * g + n
                if n == 0:
                    pool.wait_ge(MAM["delta_x_ready"], g + 1)
                pool.wait_ge(MAM["b_copied"], kk + 1)
                if due(2 * (kk - 3)):
                    pool.wait_ge(MAM["half_scanned"], 2 * (kk - 3))
                pool.tensor_tensor(mdB[:, n % 4], mdx[:, par],
                                   mBs[:, n % 4, :].rearrange("p (o t) -> p o t", o=1).to_broadcast([P, 2, GW]),
                                   ALU.mult).then_inc(MAM["delta_x_b_ready"], 1)

            def keep_state(b, n):
                pool.wait_ge(MAM["half_scanned"], 2 * (N * 2 * b + n + 1))
                pool.tensor_tensor(mhc[:, n, :], mh[:, n % 2, :, GW - 1], one[:, :], ALU.mult).then_inc(MAM["state_kept"], 1)

            def mamba_post(s, g, n):
                if n == 7:
                    pool_y_rstd(pool, 2, g)
                if n == 15 and stages > 3:
                    pool_x_rstd(pool, 3, g)

            def mamba(b, ok):
                for s in range(2):
                    g = 2 * b + s
                    for n in range(N):
                        if ok(s, 2):
                            mamba_post(s, g - 2, n)
                        if s == 1 and ok(s, 1) and n > 0:
                            keep_state(b, n - 1)
                        if ok(s, 1) and n < N - 2:
                            pool_dB(g - 1, (s - 1) % 2, n + 2)
                        if ok(s, 0):
                            mamba_prep(s, g, n)
                            if n >= N - 2:
                                pool_dB(g, s % 2, n - (N - 2))
                    if s == 1 and ok(s, 1):
                        keep_state(b, N - 1)

            if stages > 1:
                moe(1, 0)
            if stages > 2:
                stage_begins(pool, 2)
                pipeline(pool, 2, 2, mamba)
            if stages > 3:
                moe(3, 1)

        @block.scalar
        def _(act):
            def attention(b, ok):
                for s in range(TB):
                    q = s % 2
                    i = TB * b + s
                    if ok(s, 0):
                        act.wait_ge(ATT["ln_transposed"], i + 1)
                        if due(i - 1):
                            act.wait_ge(ATT["v_ready"], i - 1)
                        act.activation(azT[:, q, :], bank(0, P), ACT.Copy).then_inc(ATT["lnT_copied"], 1)
                    if ok(s, 1):
                        act.wait_ge(ATT["q_transposed"], i)
                        if due(i - 2):
                            act.wait_ge(ATT["state_added"], i - 2)
                        act.activation(aqT[:, 1 - q, :], bank(2, P), ACT.Copy).then_inc(ATT["qT_copied"], 1)
                    if ok(s, 3):
                        act.wait_ge(ATT["o_transposed"], i - 2)
                        if due(i - 4):
                            act.wait_ge(ATT["y_ready"], i - 4)
                        act.activation(aoT[:, 1 - q, :], bank(0, P), ACT.Copy).then_inc(ATT["oT_copied"], 1)
                    if ok(s, 0):
                        act.wait_ge(ATT["v_ready"], i + 1)
                        if due(i - 1):
                            act.wait_ge(ATT["kv_ready"], i - 1)
                        act.activation(av[:, q, :], bank(2, P), ACT.Copy).then_inc(ATT["v_copied"], 1)
                        act.wait_ge(ATT["min_ready"], i + 1)
                        if due(i - 1):
                            act.wait_ge(ATT["feature_ready"], i - 1)
                        act.activation(aex[:, q, :], amn[:, q, :], ACT.Exp).then_inc(ATT["exp_ready"], 1)
                    if ok(s, 3) and (s - 3) % GT == GT - 1:
                        g = (TB // GT) * b + (s - 3 - (GT - 1)) // GT
                        act.wait_ge(ATT["y_ready"], i - 2)
                        if due(ep_count(0, g - 1, 2)):
                            act.wait_ge(ep, ep_count(0, g - 1, 2))
                        act.activation(ys[:, ((s - 3) // GT) % 2], bank_tiles(7), ACT.Copy).then_inc(ys_ok, 1)
            pipeline(act, TB, 1, attention)

            def moe(st, m):
                f, B, R, buf = F[m], BLKS[m], ROWS[m], BUF[m]

                def copy_weights(g, par):
                    act.wait_ge(f["weights_transposed"], g + 1)
                    if due(R * (g - 1)):
                        act.wait_ge(f["row_ready"], R * (g - 1))
                    act.activation(buf["cwT"][0:96, par, :], bank(1, GW, 96), ACT.Copy).then_inc(f["weights_copied"], 1)

                def copy_row(g, k, j):
                    act.wait_ge(f["row_ready"], R * g + j + 1)
                    if due(B * g + k - 1 if m == 0 else B * g + k - NCH):
                        act.wait_ge(f["weighted_ready"], B * g + k - 1 if m == 0 else B * g + k - NCH)
                    act.activation(buf["cwB"][:, j % 2, :], bank(6), ACT.Copy).then_inc(f["row_copied"], 1)

                def prep(s, g, k):
                    if k == 1:
                        act.wait_ge(f["ln_transposed"], g + 1)
                        if due(g):
                            act.wait_ge(f["logits_ready"], g)
                        if due(g):
                            act.wait_ge(f["low_ln_ready"], g)
                        if due(B * (g - 1)):
                            act.wait_ge(f["up_gate_ready"], B * (g - 1))
                        act.activation(buf["zf"][:, :], bank(0), ACT.Copy)
                        act.activation(buf["z"][:, s % 2, 0, :], bank(0), ACT.Copy).then_inc(f["lnT_copied"], 1)
                    if k == (3, 5)[m]:
                        E = EXPERTS[m]
                        act.wait_ge(f["logits_shifted"], g + 1)
                        act.activation(buf["ex"][:, :, 0:E], buf["l"][:, :, 0:E], ACT.Exp).then_inc(f["exp_ready"], 1)
                    if m == 1 and k == 17:
                        copy_weights(g, s % 2)

                def post(s, g, k):
                    if k == 3:
                        act.wait_ge(f["block_added"], B * (g + 1))
                        if due(g):
                            act.wait_ge(f["y_transposed"], g)
                        act.activation(buf["yT"][:, :], bank(7), ACT.Copy).then_inc(f["yT_copied"], 1)
                    if k == 5:
                        act.wait_ge(f["y_transposed"], g + 1)
                        act.wait_ge(ep, ep_count(st, g - 2, 2))
                        act.activation(ys[:, s % 2], bank_tiles(0), ACT.Copy).then_inc(ys_ok, 1)

                def high(kk, par, at):
                    act.wait_ge(f["weighted_ready"], kk + 1)
                    if due(kk - 2):
                        act.wait_ge(f["block_added"], kk - 2)
                    act.activation(buf["a"][:, at, 0, :], buf["weighted"][:, par, :], ACT.Copy).then_inc(f["high_ready"], 1)

                def emit(b, ok):
                    for s in range(2):
                        g = 2 * b + s
                        for k in range(B):
                            kk, par = B * (g - 1) + k, (B * (s - 1) + k) % 2
                            if ok(s, 2) and k == 3:
                                post(s, g - 2, k)
                            if m == 0 and ok(s, 1) and k == 1:
                                copy_row(g - 1, 0, 0)
                            if ok(s, 1):
                                j = k if m == 0 else k // NCH
                                act.wait_ge(f["up_gate_ready"], kk + 1)
                                if due(kk - 1):
                                    act.wait_ge(f["product_ready"], kk - 1)
                                act.activation(buf["silu"][:, par, :], bank(4 + par), ACT.Silu).then_inc(f["silu_ready"], 1)
                                if k > 0 and j < R and (m == 0 or k % NCH == 0):
                                    copy_row(g - 1, k, j)
                            if ok(s, 1) and k > 0 or ok(s, 2) and k == 0:
                                high(kk - 1, 1 - par, (k - 1) % 3)
                            if ok(s, 1) and k == 0:
                                if m == 0:
                                    copy_weights(g - 1, (s - 1) % 2)
                                else:
                                    copy_row(g - 1, 0, 0)
                            if ok(s, 0):
                                prep(s, g, k)
                            if ok(s, 2) and k != 3:
                                post(s, g - 2, k)
                stage_begins(act, st)
                const_wait(act, st)
                for c in range(B // PIECE):
                    act.activation(buf["w"][:, 0, PIECE * c:PIECE * c + PIECE], wm[m][:, PIECE * c:PIECE * c + PIECE],
                                   ACT.Copy).then_inc(f["high_weights_ready"], 1)
                pipeline(act, 2, 2, emit)

            def mamba_decay(g, par, n):
                for h in range(2):
                    act.wait_ge(MAM["delta_ready"], g + 1)
                    if due(2 * (N * g + n) - 7 + h):
                        act.wait_ge(MAM["half_scanned"], 2 * (N * g + n) - 7 + h)
                    act.activation(mdec[:, n % 4, h, :], mdl[:, par, h, :], ACT.Exp,
                                   scale=aneg[:, h, n:n + 1]).then_inc(MAM["decay_ready"], 1)

            def act_norm(dst, i, bias, scale):
                scales = mr[:, scale, bass.ds(i, 1)] if scale is not None else RS[:, bass.ds(i, 1)]
                return act.activation(dst, xt(i), ACT.Identity, bias=mr[:, bias, bass.ds(i, 1)], scale=scales)

            def mamba_post(s, g, n):
                if n == 2:
                    act.wait_ge(ep, ep_count(2, g - 1, 2))
                    for t in range(GT):
                        i = act_norm(ys[:, s % 2, t, :], GT * g + t, 2, None)
                    i.then_inc(MAM["residual_ready"], 1)

            def mamba_B(g, n):
                kk = N * g + n
                act.wait_ge(MAM["b_spread"], kk + 1)
                if due(kk - 3):
                    act.wait_ge(MAM["delta_x_b_ready"], kk - 3)
                act.activation(mBs[:, n % 4, :], bank(3 + 2 * (n % 2)), ACT.Copy).then_inc(MAM["b_copied"], 1)

            def mamba_prep(s, g, n):
                if n == 0:
                    act.wait_ge(MAM["scale_step"], 8 * g + 8)
                    if due(g):
                        act.wait_ge(MAM["ln_transposed"], g)
                    for t in range(GT):
                        i = act_norm(zs[:, t, :], GT * g + t, 1, 0)
                    i.then_inc(MAM["ln_ready"], 1)
                if n == 2:
                    act.wait_ge(MAM["ln_transposed"], g + 1)
                    if due(2 * g):
                        act.wait_ge(MAM["skip_ready"], 2 * g)
                    act.activation(mxn, bank(6), ACT.Copy, scale=nw[:, 0:1]).then_inc(MAM["lnT_copied"], 1)
                if n in (4, 5):
                    h = n - 4
                    act.wait_ge(MAM["in_proj_ready"], 2 * g + h + 1)
                    act.wait_ge(MAM["carry_ready"], g + 1)
                    act.activation(mxin[:, h, TAPS - 1:TAPS - 1 + GW], bank(6 + h), ACT.Copy)
                    act.activation(mu[:, h, :], bank(6 + h), ACT.Identity, bias=cb[:, h:h + 1],
                                   scale=taps[:, h, TAPS - 1:TAPS]).then_inc(MAM["in_proj_copied"], 1)
                if n == 6:
                    if due(g - 1):
                        act.wait_ge(MAM["gated_ready"], g - 1)
                    for h in range(2):
                        act.wait_ge(MAM["skip_ready"], 2 * g + h + 1)
                        act.activation(msk[:, s % 2, h, :], bank(6 + h), ACT.Silu).then_inc(MAM["skip_silu_ready"], 1)
                    act.wait_ge(MAM["conv_step"], 6 * g + 6)
                    if due(g - 1):
                        act.wait_ge(MAM["gated_ready"], g - 1)
                    act.activation(mxs[:, s % 2], mu[:, :, :], ACT.Silu).then_inc(MAM["x_silu_ready"], 1)
                if n == 8:
                    act.wait_ge(MAM["d1_ready"], g + 1)
                    if due(2 * g):
                        act.wait_ge(MAM["d2_ready"], 2 * g)
                    act.activation(md1[0:DD, :], bank(7, GW, DD), ACT.Copy).then_inc(MAM["d1_copied"], 1)
                    act.wait_ge(MAM["bc_ready"], g + 1)
                    if due(2 * g):
                        act.wait_ge(MAM["bc_part_ready"], 2 * g)
                    if due(N * (g - 1)):
                        act.wait_ge(MAM["state_c_ready"], N * (g - 1))
                    act.activation(mbc[:, :], bank(6), ACT.Copy)
                    act.activation(mparts[:, s % 2, :], bank(6), ACT.Copy).then_inc(MAM["bc_copied"], 1)
                if n == 10:
                    if due(g):
                        act.wait_ge(MAM["delta_ready"], g)
                    for h in range(2):
                        act.wait_ge(MAM["d2_ready"], 2 * g + h + 1)
                        act.activation(mxb[:, h, :], bank(6 + h), ACT.Identity, bias=bd2[:, h:h + 1]).then_inc(MAM["d2_copied"], 1)
                if n in (10, 12):
                    c, low = (0, 64) if n == 10 else (1, 96)
                    act.wait_ge(MAM["bc_rest_ready"], 2 * g + c + 1)
                    act.activation(mparts[low:P, s % 2, :], mbc[low:P, :], ACT.Copy).then_inc(MAM["bc_part_ready"], 1)
                if n == 10:
                    act.wait_ge(MAM["d2_copied"], 2 * g + 2)
                    act.activation(mab[:, :, :], mxb[:, :, :], ACT.Abs).then_inc(MAM["abs_ready"], 1)
                if n == 11:
                    act.wait_ge(MAM["abs_ready"], g + 1)
                    act.activation(mab[:, :, :], mab[:, :, :], ACT.Exp, scale=-1.0).then_inc(MAM["exp_ready"], 1)
                    act.wait_ge(MAM["exp_ready"], g + 1)
                    act.activation(mw[:, :, :], mab[:, :, :], ACT.Copy, bias=1.0).then_inc(MAM["one_plus_exp_ready"], 1)
                    act.activation(PS[:, 6:8, :], mab[:, :, :], ACT.Ln, bias=one[:, 0:1]).then_inc(MAM["log_ready"], 1)

            def mamba(b, ok):
                for s in range(2):
                    g = 2 * b + s
                    for n in range(N):
                        if ok(s, 1):
                            if n < N - 3:
                                mamba_B(g - 1, n + 3)
                            if n < N - 2:
                                mamba_decay(g - 1, (s - 1) % 2, n + 2)
                        if ok(s, 2):
                            mamba_post(s, g - 2, n)
                        if ok(s, 0):
                            mamba_prep(s, g, n)
                            if n >= N - 3:
                                mamba_B(g, n - (N - 3))
                            if n >= N - 2:
                                mamba_decay(g, s % 2, n - (N - 2))

            if stages > 1:
                moe(1, 0)
            if stages > 2:
                const_wait(act, 2)
                act.activation(pickb[:, :], pick[:, :], ACT.Copy)
                act.activation(aneg[:, :, :], alog[:, :, :], ACT.Exp).then_inc(MAM["a_ready"], 1)
                act.wait_ge(MAM["a_ready"], 1)
                act.activation(aneg[:, :, :], aneg[:, :, :], ACT.Copy, scale=-1.0).then_inc(MAM["a_ready"], 1)
                stage_begins(act, 2)
                act.wait_ge(MAM["a_ready"], 2)
                pipeline(act, 2, 2, mamba)
            if stages > 3:
                moe(3, 1)

        @block.vector
        def _(dve):
            def dve_first_stats(g):
                dve.wait_ge(s_x[g // 2], 16)
                dve_x_stats(dve, g, ATT["x_read"], g + 1, g)
            dve_first_stats(0)
            dve_first_stats(1)

            def attention(b, ok):
                for s in range(TB):
                    q = s % 2
                    if ok(s, 0):
                        i = TB * b + s
                        if s % GT == 0:
                            dve.wait_ge(x_rstd, (TB // GT) * b + s // GT + 1)
                        if due(i - 1):
                            dve.wait_ge(ATT["ln_transposed"], i - 1)
                        dve_ln(dve, az[:, q, :], i).then_inc(ATT["ln_ready"], 1)
                    if ok(s, 1):
                        i = TB * b + s - 1
                        dve.wait_ge(ATT["exp_ready"], i + 1)
                        if due(i - 1):
                            dve.wait_ge(ATT["kv_ready"], i - 1)
                        if due(i - 1):
                            dve.wait_ge(ATT["product_ready"], i - 1)
                        dve.scalar_tensor_tensor(aphi[:, 1 - q, :], bank(1, 2 * P), 0.0, aex[:, 1 - q, :],
                                                 ALU.max, ALU.add).then_inc(ATT["feature_ready"], 1)
                    if ok(s, 2):
                        i = TB * b + s - 2
                        dve.wait_ge(ATT["kv_cumulated"], i + 1)
                        q4 = aphi[:, q, 0:P].rearrange("p (h o d) -> p h o d", h=HEADS, o=1)
                        dve.tensor_tensor(aprod.rearrange("p (h e d) -> p h e d", e=HD, d=HD),
                                          PS[:, 3:5, :].rearrange("p b (h e d) -> p (b h) e d", e=HD, d=HD),
                                          q4.to_broadcast([P, HEADS, HD, HD]), ALU.mult).then_inc(ATT["product_ready"], 1)
                        dve.wait_ge(ATT["state_added"], i + 1)
                        dve.tensor_tensor(asm, bank(5, P), heads[:, :], ALU.mult).then_inc(ATT["state_masked"], 1)
                        dve.wait_ge(ATT["product_ready"], i + 1)
                        dve.tensor_reduce(ared, aprod.rearrange("p (c d) -> p c d", d=HD), AX_X, ALU.add)\
                           .then_inc(ATT["product_summed"], 1)
                        dve.wait_ge(ATT["product_summed"], i + 1)
                        if due(i - 1):
                            dve.wait_ge(ATT["o_transposed"], i - 1)
                        if s == 2:
                            dve.tensor_copy(ao[:, q, :], ared).then_inc(ATT["o_ready"], 1)
                        else:
                            dve.tensor_tensor(ao[:, q, :], bank(6, P), ared, ALU.add).then_inc(ATT["o_ready"], 1)
                    if ok(s, 0):
                        i = TB * b + s
                        dve.wait_ge(ATT["qk_ready"], i + 1)
                        if due(i - 1):
                            dve.wait_ge(ATT["exp_ready"], i - 1)
                        dve.tensor_scalar(amn[:, q, :], bank(1, 2 * P), 0.0, None, ALU.min).then_inc(ATT["min_ready"], 1)
                    if ok(s, 4) and (s - 4) % GT == GT - 1:
                        g = (TB // GT) * b + (s - 4 - (GT - 1)) // GT
                        dve_y_stats(dve, 0, g, ((s - 4) // GT) % 2)
                    if ok(s, 5) and (s - 5) % GT == GT - 1:
                        g = (TB // GT) * b + (s - 5 - (GT - 1)) // GT
                        dve_x_update(dve, 0, g, ((s - 5) // GT) % 2)
                    if ok(s, 6) and (s - 6) % GT == GT - 1:
                        dve_new_stats(dve, 0, (TB // GT) * b + (s - 6 - (GT - 1)) // GT)
                    if isinstance(b, int) and b == 0 and s < GROUPS - 2:
                        dve_first_stats(s + 2)
            const_wait(dve, 0)
            pipeline(dve, TB, 1, attention)

            def routing(m, s, g, part):
                f, E, R, buf = F[m], EXPERTS[m], ROUTING, BUF[m]

                def v(ap):
                    return ap[:, :, 0:E]

                def cwp(i):
                    return buf["cwp"][:, :, 32 * i:32 * i + E]
                lv, ex, p, eq, l2, cw, rest = (v(buf[n]) for n in ("l", "ex", "p", "eq", "l2", "cw", "rest"))
                oh = [buf["oh"][:, j, :, 0:E] for j in range(2)]
                r_m, r_s, r_rs = buf["m"][:, :], buf["s"][:, :], buf["rs"][:, :]
                rank = rev[:, E0 - E:E0].rearrange("p (o e) -> p o e", o=1).to_broadcast([P, GT, E])
                sel = p if m == 0 else lv
                c = [((0, 0, 6, 9, 12, 14, 15, 16, 18), (0, 0, 3, 6, 9, 11, 14, 16, 18))[m][part]]

                def step(i):
                    i.then_inc(f["routing_step"], 1)
                    c[0] += 1
                    dve.wait_ge(f["routing_step"], R * g + c[0])

                def largest(sel):
                    step(dve.tensor_reduce(r_m, sel, AX_X, ALU.max))
                    step(dve.tensor_tensor(eq, sel, wide(r_m, E), ALU.is_ge))
                    step(dve.tensor_tensor(eq, eq, rank, ALU.mult))

                def first(j):
                    step(dve.tensor_reduce(r_m, eq, AX_X, ALU.max))
                    step(dve.tensor_tensor(oh[j], rank, wide(r_m, E), ALU.is_equal))
                if part == 0:
                    dve.wait_ge(f["logits_ready"], g + 1)
                    if due(g):
                        dve.wait_ge(f["weights_ready"], g)
                    dve.tensor_reduce(r_m, bank_tiles(1, E), AX_X, ALU.max).then_inc(f["maximum_ready"], 1)
                    dve.wait_ge(f["maximum_ready"], g + 1)
                    dve.tensor_tensor(lv, bank_tiles(1, E), wide(r_m, E), ALU.subtract).then_inc(f["logits_shifted"], 1)
                if part == 1:
                    dve.wait_ge(f["exp_ready"], g + 1)
                    if m == 0:
                        step(dve.tensor_reduce(r_s, ex, AX_X, ALU.add))
                        step(dve.reciprocal(r_rs, r_s))
                        step(dve.tensor_tensor(p, ex, wide(r_rs, E), ALU.mult))
                    largest(sel)
                if part == 2:
                    first(0)
                    step(dve.scalar_tensor_tensor(l2, oh[0], -1e30, sel, ALU.mult, ALU.add))
                if part == 3:
                    largest(l2)
                if part == 4:
                    first(1)
                if part == 5:
                    step(dve.tensor_tensor(eq, oh[0], oh[1], ALU.add))
                    if m == 1:
                        step(dve.tensor_tensor(eq, eq, ex, ALU.mult))
                        step(dve.tensor_reduce(r_s, eq, AX_X, ALU.add))
                if part == 6:
                    if m == 0:
                        step(dve.tensor_tensor(cw, eq, p, ALU.mult))
                    else:
                        step(dve.reciprocal(r_rs, r_s))
                        step(dve.tensor_tensor(cw, eq, wide(r_rs, E), ALU.mult))
                if part == 7:
                    if due(g):
                        dve.wait_ge(f["weights_transposed"], g)
                    step(dve.tensor_copy(cwp(0), cw))
                    step(dve.tensor_tensor(rest, cw, cwp(0), ALU.subtract))
                if part == 8:
                    step(dve.tensor_copy(cwp(1), rest))
                    step(dve.tensor_tensor(rest, rest, cwp(1), ALU.subtract))
                    dve.tensor_copy(cwp(2), rest).then_inc(f["weights_ready"], 1)
                    assert c[0] == R

            def moe(st, m):
                f, B, buf = F[m], BLKS[m], BUF[m]
                parts_at = ({2: (0,), 4: (1, 2), 5: (3, 4, 5), 7: (6, 7, 8)},
                            {3: (0,), 7: (1,), 8: (2,), 9: (3,), 10: (4,), 11: (5,), 12: (6,), 13: (7,), 14: (8,)})[m]

                def low_weights():
                    for c in range(B // PIECE):
                        piece = slice(PIECE * c, PIECE * c + PIECE)
                        dve.wait_ge(f["high_weights_ready"], c + 1)
                        dve.tensor_tensor(buf["w"][:, 1, piece], wm[m][:, piece], buf["w"][:, 0, piece].bitcast(F32),
                                          ALU.subtract).then_inc(f["low_weights_ready"], 1)

                def low(kk, par, at):
                    dve.wait_ge(f["high_ready"], kk + 1)
                    if due(kk - 2):
                        dve.wait_ge(f["block_added"], kk - 2)
                    dve.tensor_tensor(buf["a"][:, at, 1, :], buf["weighted"][:, par, :],
                                      buf["a"][:, at, 0, :].bitcast(F32), ALU.subtract).then_inc(f["low_ready"], 1)

                def emit(b, ok):
                    for s in range(2):
                        g = 2 * b + s
                        for k in range(B):
                            kk, par = B * (g - 1) + k, (B * (s - 1) + k) % 2
                            if ok(s, 0) and k == 0:
                                dve.wait_ge(x_rstd, GROUPS * st + g + 1)
                                if due(g):
                                    dve.wait_ge(f["ln_transposed"], g)
                                for t in range(GT):
                                    i = dve_ln(dve, zs[:, t, :], GT * g + t)
                                i.then_inc(f["ln_ready"], 1)
                                if isinstance(b, int) and g == 0:
                                    low_weights()
                            if ok(s, 1):
                                dve.wait_ge(f["silu_ready"], kk + 1)
                                if due(kk - 1):
                                    dve.wait_ge(f["weighted_ready"], kk - 1)
                                dve.tensor_tensor(buf["product"][:, par, :], bank(2 + par), buf["silu"][:, par, :],
                                                  ALU.mult).then_inc(f["product_ready"], 1)
                            if ok(s, 1) and k > 0 or ok(s, 2) and k == 0:
                                low(kk - 1, 1 - par, (k - 1) % 3)
                            if ok(s, 0):
                                for part in parts_at.get(k, ()):
                                    routing(m, s, g, part)
                            if ok(s, 2) and k == 6:
                                dve_y_stats(dve, st, g - 2, s % 2)
                            if ok(s, 3) and k == 0:
                                dve_x_update(dve, st, g - 3, (s - 1) % 2)
                            if ok(s, 3) and k == 1:
                                dve_new_stats(dve, st, g - 3)
                stage_begins(dve, st)
                const_wait(dve, st)
                dve.memset(buf["cwp"][:, :, :], 0.0)
                if m == 0:
                    dve.tensor_copy(pickmb[:, :], pickm[:, :])
                    dve.tensor_copy(identb[:, :], ident[:, :])
                    dve.tensor_copy(buf["wide"][:, :, :],
                                    pickm[:, :].rearrange("p (e u) -> p e u", u=1).to_broadcast([P, E0, H0]))
                dve.memset(carried[:, 15:16], 0.0).then_inc(f["constants_ready"], 1)
                dve.wait_ge(f["constants_ready"], 1)
                pipeline(dve, 2, 2, emit, longest=3)

            def mamba_prep(s, g, n):
                if n in (4, 5):
                    h = n - 4
                    dve.wait_ge(MAM["in_proj_copied"], 2 * g + h + 1)
                    for k in range(TAPS - 1):
                        dve.scalar_tensor_tensor(mu[:, h, :], mxin[:, h, k:k + GW], taps[:, h, k:k + 1], mu[:, h, :],
                                                 ALU.mult, ALU.add).then_inc(MAM["conv_step"], 1)
                        if k < TAPS - 2:
                            dve.wait_ge(MAM["conv_step"], 6 * g + 3 * h + k + 1)
                if n == 12:
                    dve.wait_ge(MAM["one_plus_exp_ready"], g + 1)
                    dve.scalar_tensor_tensor(mq[:, :, :], mw[:, :, :], -1.0, mab[:, :, :], ALU.add, ALU.subtract)\
                       .then_inc(MAM["correction_ready"], 1)
                if n == 12:
                    dve.wait_ge(MAM["log_ready"], g + 1)
                    dve.scalar_tensor_tensor(mxb[:, :, :], mxb[:, :, :], 0.0, PS[:, 6:8, :], ALU.max, ALU.add)\
                       .then_inc(MAM["delta_partly_ready"], 1)
                    dve.wait_ge(MAM["delta_partly_ready"], g + 1)
                    dve.wait_ge(MAM["correction_ready"], g + 1)
                    if due(2 * N * (g - 1)):
                        dve.wait_ge(MAM["decay_ready"], 2 * N * (g - 1))
                    dve.tensor_tensor(mdl[:, s % 2], mxb[:, :, :], mq[:, :, :], ALU.subtract).then_inc(MAM["delta_ready"], 1)

            def mamba_post(s, g, n):
                if n == 0:
                    dve.wait_ge(MAM["state_added"], N * g + N)
                    if due(g):
                        dve.wait_ge(MAM["out_proj_ready"], g)
                    dve.tensor_tensor(myg[:, :, :], PS[:, 0:2, :], msk[:, s % 2], ALU.mult).then_inc(MAM["gated_ready"], 1)
                if n == 3:
                    dve.wait_ge(MAM["residual_ready"], g + 1)
                    dve.wait_ge(MAM["out_proj_ready"], g + 1)
                    dve.tensor_tensor(ys[:, s % 2], bank_tiles(7), ys[:, s % 2], ALU.add).then_inc(ys_ok, 1)
                if n == 6:
                    dve_y_stats(dve, 2, g, s % 2)
                if n == 9:
                    dve_x_update(dve, 2, g, s % 2)
                if n == 14:
                    dve_new_stats(dve, 2, g)

            def mamba(b, ok):
                for s in range(2):
                    g = 2 * b + s
                    for n in range(N):
                        if ok(s, 1):
                            kk = N * (g - 1) + n
                            dve.wait_ge(MAM["delta_x_b_ready"], kk + 1)
                            if due(kk - 1):
                                dve.wait_ge(MAM["state_c_ready"], kk - 1)
                            if s == 1:
                                if due(N * b + n - 1):
                                    dve.wait_ge(MAM["state_kept"], N * b + n - 1)
                            elif n == 0:
                                dve.wait_ge(MAM["state_kept"], N * b)
                            for h in range(2):
                                dve.wait_ge(MAM["decay_ready"], 2 * kk + h + 1)
                                first = 0.0 if s == 1 else mhc[:, n, h:h + 1]
                                dve.tensor_tensor_scan(mh[:, n % 2, h, :], mdec[:, n % 4, h, :], mdB[:, n % 4, h, :], first,
                                                       ALU.mult, ALU.add).then_inc(MAM["half_scanned"], 1)
                            dve.wait_ge(MAM["half_scanned"], 2 * kk + 2)
                            dve.wait_ge(MAM["c_spread"], kk + 1)
                            if due(kk - 1):
                                dve.wait_ge(MAM["state_added"], kk - 1)
                            dve.tensor_tensor(mP[:, n % 2], mh[:, n % 2],
                                              bank(2 + 2 * (n % 2)).rearrange("p (o t) -> p o t", o=1).to_broadcast([P, 2, GW]),
                                              ALU.mult).then_inc(MAM["state_c_ready"], 1)
                        if ok(s, 2):
                            mamba_post(s, g - 2, n)
                        if ok(s, 0):
                            mamba_prep(s, g, n)

            if stages > 1:
                moe(1, 0)
            if stages > 2:
                stage_begins(dve, 2)
                const_wait(dve, 2)
                for h in range(2):
                    i = dve.tensor_scalar(diag[:, h, :], ident[:, :], wdd[:, h:h + 1], None, ALU.mult)
                i.then_inc(MAM["diagonal_ready"], 1)
                pipeline(dve, 2, 2, mamba)
            if stages > 3:
                moe(3, 1)

        @block.tensor
        def _(pe):
            mm = pe.matmul

            def attention(b, ok):
                for s in range(TB):
                    q = s % 2
                    if ok(s, 2):
                        i = TB * b + s - 2
                        pe.wait_ge(ATT["kv_ready"], i + 1)
                        if due(i):
                            pe.wait_ge(ATT["product_ready"], i)
                        for c in range(2):
                            r = mm(bank(3 + c), tri[:, :], akv[:, q, 512 * c:512 * c + 512], start=True, stop=True)
                        r.then_inc(ATT["kv_cumulated"], 1)
                        if s != 2:
                            pe.wait_ge(ATT["qT_copied"], i + 1)
                            pe.wait_ge(ATT["state_masked"], i)
                            pe.wait_ge(ATT["o_ready"], i)
                            mm(bank(6, P), aqT[:, q, :], asm, start=True, stop=True)
                        if due(i):
                            pe.wait_ge(ATT["state_masked"], i)
                        mm(bank(5, P), aphi[:, q, P:2 * P], av[:, q, :], start=(s == 2), stop=True,
                           skip_group_check=True).then_inc(ATT["state_added"], 1)
                    if ok(s, 0):
                        i = TB * b + s
                        pe.wait_ge(ATT["ln_ready"], i + 1)
                        if due(i):
                            pe.wait_ge(ATT["lnT_copied"], i)
                        if due(i - 3):
                            pe.wait_ge(ATT["oT_copied"], i - 3)
                        pe.transpose(bank(0, P), az[:, q, :], ident[:, :]).then_inc(ATT["ln_transposed"], 1)
                    if ok(s, 1):
                        i = TB * b + s - 1
                        pe.wait_ge(ATT["feature_ready"], i + 1)
                        pe.wait_ge(ATT["v_copied"], i + 1)
                        pe.transpose(bank(2, P), aphi[:, 1 - q, 0:P], ident[:, :]).then_inc(ATT["q_transposed"], 1)
                    if ok(s, 3):
                        i = TB * b + s - 3
                        pe.wait_ge(ATT["o_ready"], i + 1)
                        pe.wait_ge(ATT["lnT_copied"], i + 4 if not isinstance(b, int) or b < BATCHES else TILES)
                        pe.transpose(bank(0, P), ao[:, 1 - q, :], ident[:, :]).then_inc(ATT["o_transposed"], 1)
                    if ok(s, 0):
                        i = TB * b + s
                        pe.wait_ge(ATT["lnT_copied"], i + 1)
                        if due(i):
                            pe.wait_ge(ATT["feature_ready"], i)
                        mm(bank(1, 2 * P), ones[0:1, :], bqkv[0:1, 0:2 * P], start=True, stop=False)
                        mm(bank(1, 2 * P), azT[:, q, :], wqkv[:, 0:2 * P], start=False, stop=True).then_inc(ATT["qk_ready"], 1)
                        if due(i):
                            pe.wait_ge(ATT["qT_copied"], i)
                        mm(bank(2, P), ones[0:1, :], bqkv[0:1, 2 * P:3 * P], start=True, stop=False)
                        mm(bank(2, P), azT[:, q, :], wqkv[:, 2 * P:3 * P], start=False, stop=True).then_inc(ATT["v_ready"], 1)
                    if ok(s, 3):
                        i = TB * b + s - 3
                        t = (s - 3) % GT
                        pe.wait_ge(ATT["oT_copied"], i + 1)
                        if t == 0:
                            g = (TB // GT) * b + (s - 3) // GT
                            if due(g):
                                pe.wait_ge(ys_ok, g)
                        o = PS[:, 7, t * P:t * P + P]
                        mm(o, ones[0:1, :], bo[0:1, :], start=True, stop=False)
                        mm(o, aoT[:, 1 - q, :], wo[:, :], start=False, stop=True).then_inc(ATT["y_ready"], 1)
            const_wait(pe, 0)
            pe.wait_ge(pool_const, 1)
            pipeline(pe, TB, 1, attention)

            def transpose_zs(f, g, k):
                pe.wait_ge(f["ln_ready"], g + 1)
                if due(g):
                    pe.wait_ge(f["lnT_copied"], g)
                for t in range(GT):
                    r = pe.transpose(PS[:, k, t * P:t * P + P], zs[:, t, :], ident[:, :])
                r.then_inc(f["ln_transposed"], 1)

            def split_product(out, w, x, start, stop):
                mm(out, w[:, 0], x[:, 0], start=start, stop=False)
                mm(out, w[:, 1], x[:, 0], start=False, stop=False)
                return mm(out, w[:, 0], x[:, 1], start=False, stop=stop)

            def moe(st, m):
                f, B, R, buf = F[m], BLKS[m], ROWS[m], BUF[m]

                def transpose_weights(g):
                    pe.wait_ge(f["weights_ready"], g + 1)
                    for t in range(GT):
                        r = mm(PS[0:96, 1, t * P:t * P + P], buf["cwp"][:, t, :], identb[:, :], start=True, stop=True)
                    r.then_inc(f["weights_transposed"], 1)

                def spread_weights(s, g, j):
                    if j == 0:
                        pe.wait_ge(f["weights_copied"], g + 1)
                    if due(R * g + j):
                        pe.wait_ge(f["row_copied"], R * g + j)
                    if m == 0:
                        w = buf["wide"][0:96, 2 * j:2 * j + 2, :].rearrange("p e u -> p (e u)")
                    else:
                        w = pickmb[0:96, j:j + 1].to_broadcast([96, P])
                    mm(bank(6), w, buf["cwT"][0:96, (s - 1) % 2, :], start=True, stop=True).then_inc(f["row_ready"], 1)

                def prep(s, g, k):
                    if k == 1 - m:
                        pe.wait_ge(ys_ok, GROUPS * st + g - 2)
                        transpose_zs(f, g, 0)
                    if k == 2:
                        E, w = EXPERTS[m], (wg0, wg1)[m]
                        pe.wait_ge(f["lnT_copied"], g + 1)
                        if due(g):
                            pe.wait_ge(f["logits_shifted"], g)
                        if due(g):
                            pe.wait_ge(f["weights_copied"], g)
                        for t in range(GT):
                            r = mm(PS[:, 1, t * E:t * E + E], buf["zf"][:, t * P:t * P + P], w[:, :], start=True, stop=True)
                        r.then_inc(f["logits_ready"], 1)
                    if m == 1 and k == 16:
                        transpose_weights(g)

                def post(s, g, k, prep):
                    if k == 4:
                        pe.wait_ge(f["yT_copied"], g + 1)
                        pe.wait_ge(f["lnT_copied"], g + 3 if prep else GROUPS)
                        for t in range(GT):
                            r = pe.transpose(PS[:, 0, t * P:t * P + P], buf["yT"][:, t * P:t * P + P], ident[:, :])
                        r.then_inc(f["y_transposed"], 1)

                def down(kk, k, g):
                    pe.wait_ge(f["low_ready"], kk + 1)
                    if k == 0:
                        if due(g):
                            pe.wait_ge(f["yT_copied"], g)
                    split_product(bank(7), buf["w"][:, :, k, 2, :], buf["a"][:, k % 3],
                                  start=(k == 0), stop=(k == B - 1)).then_inc(f["block_added"], 1)

                def emit(b, ok):
                    for s in range(2):
                        g = 2 * b + s
                        for k in range(B):
                            kk, par = B * (g - 1) + k, (B * (s - 1) + k) % 2
                            if ok(s, 1):
                                j = k if m == 0 else k // NCH
                                if k == 0:
                                    pe.wait_ge(f["low_ln_ready"], g)
                                if m == 0 and k == 1:
                                    spread_weights(s, g - 1, 0)
                                pe.wait_ge(f["low_weights_ready"], k // PIECE + 1)
                                if due(kk - 1):
                                    pe.wait_ge(f["silu_ready"], kk - 1)
                                z = buf["z"][:, (s - 1) % 2]
                                split_product(bank(4 + par), buf["w"][:, :, k, 1, :], z, start=True, stop=True)
                                if due(kk - 1):
                                    pe.wait_ge(f["product_ready"], kk - 1)
                                split_product(bank(2 + par), buf["w"][:, :, k, 0, :], z, start=True, stop=True)\
                                   .then_inc(f["up_gate_ready"], 1)
                                if k > 0 and j < R and (m == 0 or k % NCH == 0):
                                    spread_weights(s, g - 1, j)
                            if ok(s, 1) and k >= 3:
                                down(kk - 3, k - 3, g - 1)
                            elif ok(s, 2) and k < 3:
                                down(kk - 3, B + k - 3, g - 2)
                            if ok(s, 1) and k == 0:
                                if m == 0:
                                    transpose_weights(g - 1)
                                else:
                                    spread_weights(s, g - 1, 0)
                            if ok(s, 0):
                                prep(s, g, k)
                            if ok(s, 2):
                                post(s, g - 2, k, ok(s, 0))
                stage_begins(pe, st)
                const_wait(pe, st)
                pe.wait_ge(f["constants_ready"], 1)
                pipeline(pe, 2, 2, emit)

            def row(k, par, j):
                return mm(bank(k), pickb[:, j:j + 1].to_broadcast([P, P]), mparts[:, par, :], start=True, stop=True)

            def mamba_B(g, par, n):
                kk = N * g + n
                if n == 0:
                    pe.wait_ge(MAM["bc_part_ready"], 2 * g + 2)
                if due(kk - 1):
                    pe.wait_ge(MAM["b_copied"], kk - 1)
                row(3 + 2 * (n % 2), par, n).then_inc(MAM["b_spread"], 1)

            def mamba_C(g, par, n):
                kk = N * g + n
                if due(kk - 1):
                    pe.wait_ge(MAM["state_c_ready"], kk - 1)
                row(2 + 2 * (n % 2), par, N + n).then_inc(MAM["c_spread"], 1)

            def add_state(g, par, n):
                kk = N * g + n
                pe.wait_ge(MAM["state_c_ready"], kk + 1)
                if n == 0:
                    if due(g):
                        pe.wait_ge(MAM["gated_ready"], g)
                    for h in range(2):
                        mm(bank(h), diag[:, h, :], mxs[:, par, h, :], start=True, stop=False)
                for h in range(2):
                    r = mm(bank(h), ident[:, :], mP[:, n % 2, h, :], start=False, stop=(n == N - 1))
                r.then_inc(MAM["state_added"], 1)

            def mamba_prep(s, g, n):
                par = s % 2
                if n == 1:
                    if due(g):
                        pe.wait_ge(MAM["delta_partly_ready"], g)
                    transpose_zs(MAM, g, 6)
                if n in (3, 4):
                    h = n - 3
                    pe.wait_ge(MAM["lnT_copied"], g + 1)
                    if h == 1:
                        pe.wait_ge(ys_ok, GROUPS * 2 + g - 1)
                    mm(bank(6 + h), win[:, h * P:h * P + P], mxn, start=True, stop=True).then_inc(MAM["in_proj_ready"], 1)
                if n == 5:
                    for h in range(2):
                        pe.wait_ge(MAM["in_proj_copied"], 2 * g + h + 1)
                        mm(bank(6 + h), wskip[:, h * P:h * P + P], mxn, start=True, stop=True).then_inc(MAM["skip_ready"], 1)
                if n == 7:
                    pe.wait_ge(MAM["x_silu_ready"], g + 1)
                    pe.wait_ge(MAM["skip_silu_ready"], 2 * g + 2)
                    for h in range(2):
                        r = mm(bank(7, GW, DD), wd1[:, h, :], mxs[:, par, h, :], start=(h == 0), stop=(h == 1))
                    r.then_inc(MAM["d1_ready"], 1)
                    for h in range(2):
                        r = mm(bank(6), wbc[:, h, :], mxs[:, par, h, :], start=(h == 0), stop=(h == 1))
                    r.then_inc(MAM["bc_ready"], 1)
                if n == 9:
                    pe.wait_ge(MAM["d1_copied"], g + 1)
                    pe.wait_ge(MAM["bc_copied"], g + 1)
                    for h in range(2):
                        mm(bank(6 + h), wd2[:, h * P:h * P + P], md1[0:DD, :], start=True, stop=True).then_inc(MAM["d2_ready"], 1)

            def mamba_post(s, g, n, prep):
                if n == 2:
                    pe.wait_ge(MAM["gated_ready"], g + 1)
                    pe.wait_ge(MAM["delta_partly_ready"], g + 2 if prep else GROUPS)
                    for t in range(GT):
                        for h in range(2):
                            r = mm(PS[:, 7, t * P:t * P + P], myg[:, h, t * P:t * P + P], wout[:, h, :],
                                   start=(h == 0), stop=(h == 1))
                    r.then_inc(MAM["out_proj_ready"], 1)

            def mamba(b, ok):
                for s in range(2):
                    g = 2 * b + s
                    for n in range(N):
                        if ok(s, 1):
                            if n < N - 4:
                                mamba_B(g - 1, (s - 1) % 2, n + 4)
                            if n == 0:
                                mamba_C(g - 1, (s - 1) % 2, 0)
                        if ok(s, 1) and n > 0:
                            add_state(g - 1, (s - 1) % 2, n - 1)
                        elif ok(s, 2) and n == 0:
                            add_state(g - 2, s % 2, N - 1)
                        if ok(s, 1) and n < N - 1:
                            mamba_C(g - 1, (s - 1) % 2, n + 1)
                        if ok(s, 0):
                            mamba_prep(s, g, n)
                        if ok(s, 2):
                            mamba_post(s, g - 2, n, ok(s, 0))
                        if ok(s, 0):
                            for k in {N - 3: (0,), N - 2: (1,), N - 1: (2, 3)}.get(n, ()):
                                mamba_B(g, s % 2, k)

            if stages > 1:
                moe(1, 0)
            if stages > 2:
                stage_begins(pe, 2)
                pe.wait_ge(MAM["a_ready"], 1)
                pe.wait_ge(MAM["diagonal_ready"], 1)
                pipeline(pe, 2, 2, mamba)
            if stages > 3:
                moe(3, 1)


STAGES = 4


def kernel(**inputs):
    import numpy as np
    import concourse.bacc as bacc
    from concourse import mybir as mb
    from concourse.bass_utils import run_bass_kernel_spmd

    a = {k: np.asarray(v) for k, v in inputs.items()}
    c = np.ascontiguousarray

    def halves(w):
        return c(w.reshape(2, P, -1).transpose(1, 0, 2))

    def blocks(w1, shared):
        pairs = w1.reshape(PAIRS, 2, P, H0).transpose(2, 0, 1, 3).reshape(P, PAIRS, P)
        return np.concatenate([pairs, shared[:, None, :]], axis=1)

    w1, ws1 = a["L0_ffn_W1"], a["L0_ffn_Ws1"]
    down0 = np.concatenate([a["L0_ffn_W2"].reshape(PAIRS, P, P), a["L0_ffn_Ws2"][None]], axis=0).transpose(1, 0, 2)
    wm1 = np.zeros((3, E1, NCH * P, P), np.float32)
    wm1[0, :, :H1] = a["L1_ffn_w2"]
    wm1[1, :, :H1] = a["L1_ffn_w1"]
    wm1[2, :, :H1] = a["L1_ffn_w3"].transpose(0, 2, 1)
    wm1 = wm1.reshape(3, BLK1, P, P)
    wm1 = np.stack([wm1[0].transpose(2, 0, 1), wm1[1].transpose(2, 0, 1), wm1[2].transpose(1, 0, 2)], axis=2)
    arrays = {
        "x": c(a["L0_attn_x"]),
        "ident": np.eye(P, dtype=np.float32),
        "tri": np.triu(np.ones((P, P), np.float32)),
        "heads": np.kron(np.eye(HEADS, dtype=np.float32), np.ones((HD, HD), np.float32)),
        "rev": c(np.broadcast_to(np.arange(E0, 0, -1, dtype=np.float32), (P, E0))),
        "wqkv": c(np.concatenate([a["L0_attn_Wq"].T, a["L0_attn_Wk"].T, a["L0_attn_Wv"].T], axis=1)),
        "bqkv": c(np.concatenate([a["L0_attn_bq"], a["L0_attn_bk"], a["L0_attn_bv"]])[None, :]),
        "wo": c(a["L0_attn_Wo"].T),
        "bo": c(a["L0_attn_bo"][None, :]),
        "wg0": c(a["L0_ffn_Wg"].T),
        "wm0": c(np.stack([blocks(c(w1[:, :, :H0]), ws1[:, :P]), blocks(c(w1[:, :, H0:]), ws1[:, P:]), down0], axis=2)),
        "pickm": np.concatenate([np.eye(32, E0, dtype=np.float32) * k for k in (1, 1, 1, 0)]),
        "nw": c(a["L1_attn_norm_w"][:, None]),
        "wskip": c(a["L1_attn_skip_w"].T),
        "win": c(a["L1_attn_in_w"].T),
        "taps": halves(a["L1_attn_conv_w"][:, 0, :]),
        "cb": c(a["L1_attn_conv_b"].reshape(2, P).T),
        "wd1": halves(a["L1_attn_Wd1"].T),
        "wd2": c(a["L1_attn_Wd2_w"].T),
        "bd2": c(a["L1_attn_Wd2_b"].reshape(2, P).T),
        "wbc": halves(np.concatenate([a["L1_attn_WB"].T, a["L1_attn_WC"].T] * 4, axis=1)),
        "pick": np.concatenate([np.eye(2 * N, dtype=np.float32) * k for k in (1, 0, 1, 1)]),
        "alog": halves(a["L1_attn_A_log"]),
        "wdd": c(a["L1_attn_W_D"].reshape(2, P).T),
        "wout": halves(a["L1_attn_out_w"].T),
        "wg1": c(a["L1_ffn_gate_w"].T),
        "wm1": c(wm1),
    }
    nc = bacc.Bacc("TRN2", target_bir_lowering=False, num_devices=1)
    aps = {n: nc.dram_tensor("in_" + n, v.shape, mb.dt.from_np(v.dtype), kind="ExternalInput").ap()
           for n, v in arrays.items()}
    out = nc.dram_tensor("out_x", a["L0_attn_x"].shape, mb.dt.float32, kind="ExternalOutput").ap()
    program(nc, aps, out, STAGES)
    r = run_bass_kernel_spmd(nc, [{"in_" + n: v for n, v in arrays.items()}], core_ids=[0])
    return r.results[0]["out_x"]
```
